# Optimizing a Trainium2 kernel written in Bass

```python
import numpy as np
import jax
import jax.numpy as jnp

def _softmax(x, axis=-1):
    return jax.nn.softmax(x, axis=axis)

def _gelu(x):
    return jax.nn.gelu(x, approximate=True)

def _silu(x):
    return jax.nn.silu(x)

def _sigmoid(x):
    return jax.nn.sigmoid(x)

def _layernorm(x, axis=-1, eps=1e-05):
    m = jnp.mean(x, axis=axis, keepdims=True)
    v = jnp.var(x, axis=axis, keepdims=True)
    return (x - m) / jnp.sqrt(v + eps)

def _scatter_add(tgt, idx, src, axis=0):
    return tgt.at[idx].add(src)

def _segment_sum(src, seg, n):
    return jax.ops.segment_sum(src, seg, n)
kernel_name = 'mk_seq_preln_d1_jaxref_r4_f49497'

def setup_inputs(seed: int=0):
    np.random.seed(seed)
    _w = jnp.asarray

    def _L0_attn_setup():
        import jax, jax.numpy as jnp
        import numpy as np
        D_MODEL = 512
        GN_EPS = 1e-05
        key = jax.random.key(seed)
        ks = jax.random.split(key, 6)
        B, T, D = (4, 512, D_MODEL)
        s = 1.0 / np.sqrt(D)
        return {'x': jax.random.normal(ks[0], (B, T, D), dtype=jnp.float32), 'Wr': jax.random.normal(ks[1], (D, D), dtype=jnp.float32) * s, 'Wk': jax.random.normal(ks[2], (D, D), dtype=jnp.float32) * s, 'Wv': jax.random.normal(ks[3], (D, D), dtype=jnp.float32) * s, 'Wo': jax.random.normal(ks[4], (D, D), dtype=jnp.float32) * s, 'decay': jnp.ones((D,), dtype=jnp.float32) * 0.99, 'gn_weight': jnp.ones((D,), dtype=jnp.float32), 'gn_bias': jnp.zeros((D,), dtype=jnp.float32)}
    _L0_attn_in = _L0_attn_setup()

    def _L0_ffn_setup():
        import jax, jax.numpy as jnp
        import numpy as np
        E = 64
        K = 4
        H = 512
        I = 384
        C = 64
        B, S = (1, 512)
        key = jax.random.key(seed)
        ks = jax.random.split(key, 8)
        sh = 1.0 / np.sqrt(H).astype(np.float32)
        si = 1.0 / np.sqrt(I).astype(np.float32)
        return {'x': jax.random.normal(ks[0], (B, S, H), jnp.float32), 'w_router': jax.random.normal(ks[1], (E, H), jnp.float32) * sh, 'w_gate': jax.random.normal(ks[2], (E, H, I), jnp.float32) * sh, 'w_up': jax.random.normal(ks[3], (E, H, I), jnp.float32) * sh, 'w_down': jax.random.normal(ks[4], (E, I, H), jnp.float32) * si, 'w_sh_gate': jax.random.normal(ks[5], (H, I), jnp.float32) * sh, 'w_sh_up': jax.random.normal(ks[6], (H, I), jnp.float32) * sh, 'w_sh_down': jax.random.normal(ks[7], (I, H), jnp.float32) * si}
    _L0_ffn_in = _L0_ffn_setup()
    _d = {'L0_attn_x': _L0_attn_in['x'], 'L0_attn_Wr': _L0_attn_in['Wr'], 'L0_attn_Wk': _L0_attn_in['Wk'], 'L0_attn_Wv': _L0_attn_in['Wv'], 'L0_attn_Wo': _L0_attn_in['Wo'], 'L0_attn_decay': _L0_attn_in['decay'], 'L0_attn_gn_weight': _L0_attn_in['gn_weight'], 'L0_attn_gn_bias': _L0_attn_in['gn_bias'], 'L0_ffn_w_router': _L0_ffn_in['w_router'], 'L0_ffn_w_gate': _L0_ffn_in['w_gate'], 'L0_ffn_w_up': _L0_ffn_in['w_up'], 'L0_ffn_w_down': _L0_ffn_in['w_down'], 'L0_ffn_w_sh_gate': _L0_ffn_in['w_sh_gate'], 'L0_ffn_w_sh_up': _L0_ffn_in['w_sh_up'], 'L0_ffn_w_sh_down': _L0_ffn_in['w_sh_down']}
    _x0 = _d['L0_attn_x']
    _d['L0_attn_x'] = jax.random.normal(jax.random.fold_in(jax.random.key(seed), 1), (2, 1024, 512), dtype=_x0.dtype)
    del _x0
    return _d

def reference(L0_attn_x, L0_attn_Wr, L0_attn_Wk, L0_attn_Wv, L0_attn_Wo, L0_attn_decay, L0_attn_gn_weight, L0_attn_gn_bias, L0_ffn_w_router, L0_ffn_w_gate, L0_ffn_w_up, L0_ffn_w_down, L0_ffn_w_sh_gate, L0_ffn_w_sh_up, L0_ffn_w_sh_down):

    def _L0_attn_ref(x, Wr, Wk, Wv, Wo, decay, gn_weight, gn_bias):
        import jax, jax.numpy as jnp
        import numpy as np
        D_MODEL = 512
        GN_EPS = 1e-05
        B, T, D = x.shape
        r = jax.nn.sigmoid(jnp.einsum('btd,ed->bte', x, Wr))
        k = jnp.einsum('btd,ed->bte', x, Wk)
        v = jnp.einsum('btd,ed->bte', x, Wv)
        d = jax.nn.sigmoid(decay)
        log_decay = jnp.log(jnp.clip(d, 1e-07, None))
        pos = jnp.arange(T, dtype=x.dtype)
        scale = jnp.exp(pos[:, None] * log_decay[None, :])
        scaled = k * v / jnp.clip(scale, 1e-10, None)[None]
        state = jnp.cumsum(scaled, axis=1) * scale[None]
        out = r * state
        mean = jnp.mean(out, axis=(1, 2), keepdims=True)
        var = jnp.mean(jnp.square(out - mean), axis=(1, 2), keepdims=True)
        normed = (out - mean) * jax.lax.rsqrt(var + GN_EPS)
        normed = normed * gn_weight + gn_bias
        return jnp.einsum('btd,ed->bte', normed, Wo)

    def _L0_ffn_ref(x, w_router, w_gate, w_up, w_down, w_sh_gate, w_sh_up, w_sh_down):
        import jax, jax.numpy as jnp
        import numpy as np
        E = 64
        K = 4
        H = 512
        I = 384
        C = 64
        B, S = (1, 512)
        b, s, h = x.shape
        xf = x.reshape(-1, h)
        T = xf.shape[0]
        P = T * K
        logits = xf @ w_router.T
        top_vals, top_idx = jax.lax.top_k(logits, K)
        w_tok = jax.nn.softmax(top_vals.astype(jnp.float32), axis=-1)
        e_flat = top_idx.reshape(-1)
        tok_flat = jnp.repeat(jnp.arange(T), K)
        w_flat = w_tok.reshape(-1)
        order = jnp.argsort(e_flat)
        tok_s = tok_flat[order]
        w_s = w_flat[order]
        counts = jnp.zeros((E,), jnp.int32).at[e_flat].add(1)
        offsets = jnp.cumsum(counts) - counts
        pos = offsets[:, None] + jnp.arange(C)[None, :]
        valid = jnp.arange(C)[None, :] < counts[:, None]
        pos_c = jnp.clip(pos, 0, P - 1)
        tok_ec = tok_s[pos_c]
        w_ec = jnp.where(valid, w_s[pos_c], 0.0)
        x_ec = xf[tok_ec]
        g = jax.nn.silu(jnp.einsum('ech,ehi->eci', x_ec, w_gate))
        u = jnp.einsum('ech,ehi->eci', x_ec, w_up)
        y = jnp.einsum('eci,eih->ech', g * u, w_down)
        contrib = (y * w_ec[..., None]).reshape(-1, h)
        combined = jnp.zeros_like(xf).at[tok_ec.reshape(-1)].add(contrib)
        sg = jax.nn.silu(xf @ w_sh_gate)
        su = xf @ w_sh_up
        combined = combined + sg * su @ w_sh_down
        return combined.reshape(b, s, h)
    x = L0_attn_x
    x = x + _L0_attn_ref(_layernorm(x, axis=-1), L0_attn_Wr, L0_attn_Wk, L0_attn_Wv, L0_attn_Wo, L0_attn_decay, L0_attn_gn_weight, L0_attn_gn_bias)
    x = x + _L0_ffn_ref(_layernorm(x, axis=-1), L0_ffn_w_router, L0_ffn_w_gate, L0_ffn_w_up, L0_ffn_w_down, L0_ffn_w_sh_gate, L0_ffn_w_sh_up, L0_ffn_w_sh_down)
    return x

_drawn_inputs = setup_inputs


def setup_inputs(seed=0):
    import zlib

    import numpy as np

    out = dict(_drawn_inputs(seed))
    spreads = {'L0_attn_decay': (0.9900000095367432, 0.2),
     'L0_attn_gn_weight': (1.0, 0.2),
     'L0_attn_gn_bias': (0.0, 0.1)}
    factors = {}
    for name, (base, spread) in spreads.items():
        noise = np.random.default_rng([zlib.crc32(name.encode()), seed]).standard_normal(out[name].shape)
        drawn = base * np.exp(spread * noise) if base else spread * noise
        out[name] = jnp.asarray(drawn.astype(out[name].dtype))
    for name, factor in factors.items():
        out[name] = (out[name] * factor).astype(out[name].dtype)
    return out
```

```python
from contextlib import ExitStack

import concourse.bass as bass
from concourse import mybir

F32 = mybir.dt.float32
U32 = mybir.dt.uint32
I32 = mybir.dt.int32
ALU = mybir.AluOpType
ACT = mybir.ActivationFunctionType
AX = mybir.AxisListType

P = 128
SEQS, T, D = 2, 1024, 512
TOKENS = SEQS * T
KC = D // P
TILES = T // P
HALF = 512
HALVES = T // HALF
E, TOPK, I, C = 64, 4, 384, 64
IC = I // P
ROW = D + E
LN_EPS = 1e-5
SENTINEL, TAKEN = -3.0e38, -3.3e38
NORMS = 2 * TILES + 1
MEMBER = 4096.0
GROUPS = E // 4


def moe_block(nc, x, wr, wk, wv, wo, decay, gn_w, gn_b, w_router, w_gate, w_up, w_down,
              sh_gate, sh_up, sh_down, out):
    xw_dram = nc.dram_tensor("xw_dram", [TOKENS, ROW], F32, kind="Internal").ap()
    xt_dram = nc.dram_tensor("xt_dram", [TOKENS // P, P, D], F32, kind="Internal").ap()

    with ExitStack() as ctx:
        def sb(name, shape, dt=F32):
            return ctx.enter_context(nc.sbuf_tensor(name, shape, dt))

        def sem(name):
            return ctx.enter_context(nc.semaphore(name))

        def sem2(name):
            return [sem(f"{name}{u}") for u in range(2)]

        bank = [ctx.enter_context(nc.psum_tensor(f"bank{i}", [P, 512], F32)) for i in range(8)]
        ps_r, ps_k, ps_v, ps_t = bank[0:2], bank[2:4], bank[4:6], bank[6:8]
        ps_y, ps_l, ps_m = ps_r, ps_k, ps_v
        ps_g, ps_u, ps_xt, ps_ht, ps_d = bank[0:2], bank[2:4], bank[4], bank[5], bank[6:8]

        ident = sb("ident", [P, P])
        mean_mat = sb("mean_mat", [P, P])
        ones = sb("ones", [P, HALF])
        ramp = sb("ramp", [E, T])
        proj_sb = sb("proj_sb", [P, 4, KC * D])
        wr_sb, wk_sb, wv_sb, wo_sb = (proj_sb[:, n, :].rearrange("p (c n) -> p c n", c=KC) for n in range(4))
        router_sb = sb("router_sb", [P, KC, E])
        dec = sb("dec", [P, 4, KC])
        gnw_sb, gnb_sb = sb("gnw_sb", [P, KC]), sb("gnb_sb", [P, KC])
        scale, inv = sb("scale", [P, KC, T]), sb("inv", [P, HALF])
        xin = [sb(f"xin{u}", [P, D]) for u in range(2)]
        stats = sb("stats", [P, 6])
        mv = [sb(f"mv{u}", [P, 2]) for u in range(2)]
        var_eps = [sb(f"var_eps{u}", [P, 1]) for u in range(2)]
        rstd = [sb(f"rstd{u}", [P, 1]) for u in range(2)]
        minus_half = sb("minus_half", [P, 1])
        xn = [sb(f"xn{u}", [P, D]) for u in range(2)]
        xnT = sb("xnT", [P, KC, T])
        r_sb = [sb(f"r_sb{u}", [P, HALF]) for u in range(2)]
        v_sb = [sb(f"v_sb{u}", [P, HALF]) for u in range(2)]
        kv = sb("kv", [P, HALF])
        state = sb("state", [P, T])
        outT = sb("outT", [P, KC, T])
        pos_i = outT[:, 0, :].bitcast(I32)
        gstats = sb("gstats", [P, KC * HALVES, 6])
        gmv = sb("gmv", [P, 2])
        gtmp = sb("gtmp", [P, 4])
        gA, gB = sb("gA", [P, KC]), sb("gB", [P, KC])
        x2 = [sb(f"x2_{u}", [P, D]) for u in range(2)]
        xw = xn
        xwT = [sb(f"xwT{u}", [P, KC, P]) for u in range(2)]
        logits = sb("logits", [P, TILES, E + 4])
        top8 = sb("top8", [P, TILES, 8])
        pick8 = sb("pick8", [P, TILES, 8])
        picked = sb("picked", [P, TILES, E + 4])
        mask = sb("mask", [P, TILES, E])
        wgt = sb("wgt", [P, TILES, E])
        wsum = sb("wsum", [P, TILES])
        key = state[0:E, :]
        cand_b = sb("cand_b", [E, C])
        cand = sb("cand", [E, SEQS * C])
        slots = sb("slots", [E, C])
        bump = sb("bump", [E, C])
        tok2 = sb("tok2", [E, 2, C])
        idx = sb("idx", [P, E], U32)
        pair_idx = sb("pair_idx", [P, E // 2], U32)
        w_sb = sb("w_sb", [P, 2, 2, 3, KC * I])
        gidx = [sb(f"gidx{u}", [P, 1], U32) for u in range(2)]
        sidx = [sb(f"sidx{u}", [C, 1], U32) for u in range(2)]
        wcol = [sb(f"wcol{u}", [P, 1]) for u in range(2)]

        def carve(tile, sizes):
            flat, at, views = tile[:, :, :].rearrange("p a b -> p (a b)"), 0, []
            for n in sizes:
                views.append(flat[:, at:at + n])
                at += n
            return views

        *xT, xS, sg0, sg1, sg2, gu0, gu1, gu2 = carve(scale, [D] * 3 + [I] * 6)
        sg, gu = [sg0, sg1, sg2], [gu0, gu1, gu2]
        *guT, yA0, yA1, yB0, yB1, yS = carve(xnT, [I] * 3 + [D] * 5)
        yA, yB = [yA0[0:C, :], yA1[0:C, :]], [yB0[0:C, :], yB1[0:C, :]]
        xg = carve(outT, [ROW] * 2)
        xT = [t.rearrange("p (c t) -> p c t", c=KC) for t in xT]
        guT = [t.rearrange("p (c t) -> p c t", c=IC) for t in guT]
        xS = xS.rearrange("p (c t) -> p c t", c=KC)

        def gate_up(u, e, which):
            return w_sb[:, u, e, which, :].rearrange("p (c n) -> p c n", c=KC)

        def down(u, e):
            return w_sb[:, u, e, 2, :].rearrange("p (c n) -> p c n", c=IC)

        sh_gu = [proj_sb[:, w, 0:KC * I].rearrange("p (c n) -> p c n", c=KC) for w in range(2)]
        sh_dn = proj_sb[:, 2, 0:KC * I].rearrange("p (c n) -> p c n", c=IC)

        def chunk(ap, c, n=KC):
            return ap.rearrange("p (m c) -> p c m", c=n)[:, c, :]

        vectors_in = sem("vectors_in")
        params_in = sem("params_in")
        params2_in = sem("params2_in")
        sh_full = sem("sh_full")
        const_ready = sem("const_ready")
        setup = sem("setup")
        xin_full = sem2("xin_full")
        xn_ready = sem2("xn_ready")
        xn_turned = sem2("xn_turned")
        xnT_ready = sem2("xnT_ready")
        r_ready, k_ready, v_ready = sem2("r_ready"), sem2("k_ready"), sem2("v_ready")
        sig_done, vcopy_done = sem2("sig_done"), sem2("vcopy_done")
        kv_done, out_done = sem2("kv_done"), sem2("out_done")
        var_ready, rstd_ready = sem("var_ready"), sem("rstd_ready")
        dve_seq = sem("dve_seq")
        pool_seq = sem("pool_seq")
        gpart_ready = sem("gpart_ready")
        gmean_ready = sem("gmean_ready")
        gn_applied = sem("gn_applied")
        xc_full = sem2("xc_full")
        y_ready = sem2("y_ready")
        x2_done = sem2("x2_done")
        xw_ready = sem2("xw_ready")
        xw_turned = sem2("xw_turned")
        xwT_ready = sem2("xwT_ready")
        logit_ready, logit_copied = sem2("logit_ready"), sem2("logit_copied")
        x2_stored, xw_stored, xwT_stored = sem2("x2_stored"), sem2("xw_stored"), sem2("xwT_stored")
        diff_ready = sem("diff_ready")
        exp_done = sem("exp_done")
        mask_ready = sem("mask_ready")
        wgt_ready = sem("wgt_ready")
        wgt_stored = sem("wgt_stored")
        mask_turned = sem("mask_turned")
        keys_made = sem("keys_made")
        tok_ready = sem("tok_ready")
        tok_turned = sem("tok_turned")
        idx_ready = sem("idx_ready")
        w_full = [[sem(f"w_full{u}_{k}") for k in range(3)] for u in range(2)]
        xg_full = sem2("xg_full")
        xg_turned = sem2("xg_turned")
        xT_ready = sem2("xT_ready")
        wcol_ready = sem2("wcol_ready")
        xS_full = sem("xS_full")
        g_ready = [sem(f"g_ready{u}") for u in range(3)]
        u_ready = [sem(f"u_ready{u}") for u in range(3)]
        sg_ready = [sem(f"sg_ready{u}") for u in range(3)]
        gu_ready = [sem(f"gu_ready{u}") for u in range(3)]
        gu_turned = [sem(f"gu_turned{u}") for u in range(3)]
        guT_ready = [sem(f"guT_ready{u}") for u in range(3)]
        d_ready = [sem(f"d_ready{u}") for u in range(3)]
        yA_ready, yB_ready, yS_ready = sem2("yA_ready"), sem2("yB_ready"), sem("yS_ready")
        added = sem("added")

        ADDS = 16 * 5

        def token_rows(b, i):
            return bass.ds(b * T + i * P, P)

        class Steps:

            def __init__(self, eng, s):
                self.eng, self.s, self.base, self.n = eng, s, 0, 0

            def then(self, ins, apart=False):
                self.n += 1
                ins.then_inc(self.s, 1)
                self.eng.wait_ge(self.s, self.base + self.n)
                if apart:
                    self.eng.nop(nofuse=True)

            def loop(self, i, per, before):
                self.base, self.n = i * per + before, 0

        block = ctx.enter_context(nc.Block())

        @block.sync
        def _(sp):
            def load_x(full, b, i, normed, summed):
                sp.wait_ge(xn_ready[i % 2], normed)
                sp.wait_ge(x2_done[i % 2], summed)
                sp.dma_start(xin[i % 2][:, :], x[token_rows(b, i), :]).then_inc(full[i % 2], 16)

            def load_pair(j, u):
                for k, w in enumerate((w_gate, w_up, w_down)):
                    sp.wait_ge((g_ready[u], u_ready[u], d_ready[u])[k], j)
                    for e in range(2):
                        sp.dma_start(w_sb[:, u, e, k, :], w[bass.ds(j * 4 + u * 2 + e, 1)].rearrange(
                            "a (p c) n -> (a p) (c n)", p=P)).then_inc(w_full[u][k], 16)

            sp.dma_start(dec[:, 0, :], decay.rearrange("(p c) -> p c", c=KC)).then_inc(vectors_in, 16)
            sp.dma_start(gnw_sb[:, :], gn_w.rearrange("(p c) -> p c", c=KC)).then_inc(vectors_in, 16)
            sp.dma_start(gnb_sb[:, :], gn_b.rearrange("(p c) -> p c", c=KC)).then_inc(vectors_in, 16)

            for u in range(2):
                load_pair(0, u)
            with sp.Fori(0, SEQS) as b:
                for i in range(TILES):
                    load_x(xin_full, b, i, b * (TILES // 2) + i // 2, b * (TILES // 2))
                for i in range(TILES):
                    load_x(xc_full, b, i, (b + 1) * (TILES // 2), b * (TILES // 2) + i // 2)

            sp.wait_ge(k_ready[1], SEQS * KC)
            for k, w in enumerate((sh_gate, sh_up, sh_down)):
                sp.dma_start(proj_sb[:, k, 0:KC * I], w.rearrange("(p c) n -> p (c n)", p=P)).then_inc(sh_full, 16)
            sp.wait_ge(idx_ready, 3)
            for u in range(2):
                sp.wait_ge(xwT_stored[u], 16 * SEQS * TILES // 2)
            with sp.Fori(0, GROUPS - 1) as j:
                sp.wait_ge(u_ready[2], j)
                sp.dma_start(xS[:, :, :].rearrange("p c t -> p (c t)"),
                             xt_dram[bass.ds(j, 1)].rearrange("a p n -> (a p) n")).then_inc(xS_full, 16)
                for u in range(2):
                    load_pair(j + 1, u)
            sp.wait_ge(u_ready[2], GROUPS - 1)
            sp.dma_start(xS[:, :, :].rearrange("p c t -> p (c t)"), xt_dram[GROUPS - 1]).then_inc(xS_full, 16)

        @block.gpsimd
        def _(pool):
            seq = Steps(pool, pool_seq)
            seq.then(pool.memset(ident[:, :], 0.0))
            seq.then(pool.affine_select(out=ident[:, :], in_=ident[:, :], compare_op=ALU.not_equal, fill=1.0,
                                        base=0, pattern=[[-1, P]], channel_multiplier=1))
            pool.memset(mean_mat[:, :], 1.0 / P)
            pool.memset(ones[:, :], 1.0)
            pool.memset(minus_half[:, :], -0.5)
            pool.memset(logits[:, :, E:], SENTINEL)
            pool.memset(pick8[:, :, TOPK:], SENTINEL)
            pool.iota(pos_i[:, :], pattern=[[1, T]], base=0, channel_multiplier=0).then_inc(const_ready, 1)
            pool.iota(ramp[:, :], pattern=[[-1, T]], base=TOKENS, channel_multiplier=0,
                      allow_small_or_imprecise_dtypes=True).then_inc(const_ready, 1)
            pool.dma_start(wr_sb[:, :, :], wr.rearrange("(p c) n -> p c n", c=KC)).then_inc(params_in, 16)
            pool.dma_start(wv_sb[:, :, :], wv.rearrange("(p c) n -> p c n", c=KC)).then_inc(params_in, 16)
            pool.dma_start(wk_sb[:, :, :], wk.rearrange("(p c) n -> p c n", c=KC)).then_inc(params_in, 16)
            pool.dma_start(wo_sb[:, :, :], wo.rearrange("(p c) n -> p c n", c=KC)).then_inc(params2_in, 16)
            pool.dma_start(router_sb[:, :, :], w_router.rearrange("(p c) n -> p c n", c=KC)).then_inc(params2_in, 16)

            def power(b, n):
                pool.wait_ge(var_ready, b * NORMS + n + 1)
                pool.tensor_tensor(rstd[n % 2][:, :], var_eps[n % 2][:, :], minus_half[:, :],
                                   ALU.pow).then_inc(rstd_ready, 1)

            def store_turned(b, i):
                u, m = i % 2, b * (TILES // 2) + i // 2
                pool.wait_ge(xwT_ready[u], m + 1)
                pool.dma_start(xt_dram[bass.ds(b * TILES + i, 1)].rearrange("a p n -> (a p) n"),
                               xwT[u][:, :, :].rearrange("p c t -> p (c t)")).then_inc(xwT_stored[u], 16)

            with pool.Fori(0, SEQS) as b:
                for n in range(TILES + 1):
                    power(b, n)
                for i in range(TILES):
                    u, m = i % 2, b * (TILES // 2) + i // 2
                    power(b, TILES + 1 + i)
                    if i:
                        store_turned(b, i - 1)
                    pool.wait_ge(x2_done[u], m + 1)
                    pool.dma_start(out[token_rows(b, i), :], x2[u][:, :]).then_inc(x2_stored[u], 16)
                    pool.wait_ge(xw_ready[u], m + 1)
                    pool.dma_start(xw_dram[token_rows(b, i), 0:D], xw[u][:, :]).then_inc(xw_stored[u], 16)
                store_turned(b, TILES - 1)
                pool.wait_ge(wgt_ready, b + 1)
                pool.dma_start(xw_dram[bass.ds(b * T, T), D:ROW].rearrange("(i p) e -> p i e", p=P),
                               wgt[:, :, :]).then_inc(wgt_stored, 16)

            def gather(j, u):
                pool.wait_ge(xg_turned[u], j)
                pool.wait_ge(wcol_ready[u], j)
                seq.then(pool.tensor_copy(gidx[u][:, :], pair_idx[:, bass.ds(j * 2 + u, 1)]), apart=True)
                pool.indirect_dma_start(out=xg[u][:, :], out_offset=None, in_=xw_dram[:, :],
                                        in_offset=bass.IndirectOffsetOnAxis(ap=gidx[u][:, :], axis=0),
                                        ).then_inc(xg_full[u], 16)

            def add_group(j):
                n = 0
                for u in range(2):
                    for e, (y, ready) in enumerate(((yA, yA_ready), (yB, yB_ready))):
                        pool.wait_ge(ready[u], j + 1)
                        pool.wait_ge(added, j * ADDS + n)
                        seq.then(pool.tensor_copy(sidx[e][:, :], idx[0:C, bass.ds(j * 4 + u * 2 + e, 1)]), apart=True)
                        pool.indirect_dma_start(out=out[:, :],
                                                out_offset=bass.IndirectOffsetOnAxis(ap=sidx[e][:, :], axis=0),
                                                in_=y[u][:, :], in_offset=None,
                                                compute_op=ALU.add).then_inc(added, 16)
                        n += 16
                pool.wait_ge(yS_ready, j + 1)
                pool.wait_ge(added, j * ADDS + n)
                pool.dma_start(out[bass.ds(j * P, P), :], yS[:, :], accum_op=ALU.add).then_inc(added, 16)

            for u in range(2):
                pool.wait_ge(x2_stored[u], 16 * TOKENS // P // 2)
                pool.wait_ge(xw_stored[u], 16 * TOKENS // P // 2)
            pool.wait_ge(wgt_stored, 16 * SEQS)
            pool.wait_ge(idx_ready, 3)
            for u in range(2):
                gather(0, u)
            before = seq.n
            with pool.Fori(0, GROUPS - 1) as j:
                seq.loop(j, 6, before)
                for u in range(2):
                    gather(j + 1, u)
                add_group(j)
            seq.base, seq.n = 0, before + 6 * (GROUPS - 1)
            add_group(GROUPS - 1)
            pool.wait_ge(added, GROUPS * ADDS)

        @block.scalar
        def _(act):
            act.wait_ge(vectors_in, 16 * 3)
            act.activation(dec[:, 1, :], dec[:, 0, :], ACT.Sigmoid).then_inc(setup, 1)
            act.wait_ge(setup, 2)
            act.activation(dec[:, 3, :], dec[:, 2, :], ACT.Ln).then_inc(setup, 1)
            act.wait_ge(setup, 3)
            act.wait_ge(const_ready, 1)
            for c in range(KC):
                act.activation(scale[:, c, :], pos_i[:, :], ACT.Exp, scale=dec[:, 3, c:c + 1]).then_inc(setup, 1)

            with act.Fori(0, SEQS) as b:
                m0 = b * (TILES // 2)
                for i in range(TILES):
                    u, m = i % 2, m0 + i // 2
                    act.wait_ge(xn_turned[u], m + 1)
                    act.activation(xnT[:, :, i * P:(i + 1) * P], ps_t[u][:, :].rearrange("p (c t) -> p c t", c=KC),
                                   ACT.Copy).then_inc(xnT_ready[u], 1)
                for c in range(KC):
                    for h in range(HALVES):
                        m = b * KC + c
                        act.wait_ge(r_ready[h], m + 1)
                        act.wait_ge(out_done[h], m)
                        act.activation(r_sb[h][:, :], ps_r[h][:, :], ACT.Sigmoid).then_inc(sig_done[h], 1)
                        act.wait_ge(v_ready[h], m + 1)
                        act.wait_ge(kv_done[h], m)
                        act.activation(v_sb[h][:, :], ps_v[h][:, :], ACT.Copy).then_inc(vcopy_done[h], 1)
                for i in range(TILES):
                    u, m = i % 2, m0 + i // 2
                    act.wait_ge(xw_turned[u], m + 1)
                    act.wait_ge(logit_ready[u], m)
                    act.wait_ge(xwT_stored[u], 16 * m)
                    act.activation(xwT[u][:, :, :], ps_t[u][:, :].rearrange("p (c t) -> p c t", c=KC),
                                   ACT.Copy).then_inc(xwT_ready[u], 1)
                act.wait_ge(diff_ready, b + 1)
                act.activation(wgt[:, :, :], wgt[:, :, :], ACT.Exp).then_inc(exp_done, 1)

            with act.Fori(0, GROUPS) as j:
                def silu(n, u):
                    act.wait_ge(g_ready[n], j + 1)
                    act.wait_ge(gu_ready[n], j)
                    act.activation(sg[n][:, :], ps_g[u][:, 0:I], ACT.Silu).then_inc(sg_ready[n], 1)

                for u in range(2):
                    act.wait_ge(xg_turned[u], j + 1)
                    act.wait_ge(u_ready[u], j)
                    act.activation(xT[u][:, :, :], ps_xt[:, :].rearrange("p (c t) -> p c t", c=KC),
                                   ACT.Copy).then_inc(xT_ready[u], 1)
                    silu(u, u)
                silu(2, 0)
                act.wait_ge(added, j * ADDS)
                for u in range(2):
                    act.wait_ge(d_ready[u], j + 1)
                    act.wait_ge(wcol_ready[u], j + 1)
                    act.activation(yA[u][:, :], ps_d[u][0:C, :], ACT.Copy, scale=wcol[u][0:C, :]).then_inc(yA_ready[u], 1)
                act.wait_ge(d_ready[2], j + 1)
                act.activation(yS[:, :], ps_d[0][:, :], ACT.Copy).then_inc(yS_ready, 1)

        @block.vector
        def _(dve):
            seq = Steps(dve, dve_seq)

            norms = [0, 0]

            def need_rstd(b, var):
                u = norms[0] % 2
                dve.tensor_scalar(var_eps[u][:, :], var, LN_EPS, None, ALU.add).then_inc(var_ready, 1)
                norms[0] += 1

            def take_rstd(b):
                u = norms[1] % 2
                norms[1] += 1
                dve.wait_ge(rstd_ready, b * NORMS + norms[1])
                return rstd[u]

            def row_stats(b, src):
                u = norms[0] % 2
                seq.then(dve.bn_stats(stats[:, :], src[:, :]), apart=True)
                seq.then(dve.bn_aggr(mv[u][:, :], stats[:, :]))
                need_rstd(b, mv[u][:, 1:2])

            def normalise(b, src, dst):
                u = norms[1] % 2
                r = take_rstd(b)
                return dve.tensor_scalar(dst[:, :], src[:, :], mv[u][:, 0:1], r[:, :], ALU.subtract, ALU.mult)

            dve.wait_ge(setup, 1)
            dve.tensor_scalar(dec[:, 2, :], dec[:, 1, :], 1e-7, None, ALU.max).then_inc(setup, 1)
            dve.wait_ge(setup, 3 + KC)
            dve.wait_ge(vectors_in, 16 * 3)
            before = seq.n

            def phase1(b):
                norms[0] = norms[1] = 0
                for i in range(TILES + 1):
                    if i < TILES:
                        dve.wait_ge(xin_full[i % 2], 16 * (b * (TILES // 2) + i // 2 + 1))
                        row_stats(b, xin[i % 2])
                    if i == 0:
                        continue
                    u, m = (i - 1) % 2, b * (TILES // 2) + (i - 1) // 2
                    dve.wait_ge(xn_turned[u], m)
                    dve.wait_ge(xw_turned[u], b * (TILES // 2))
                    dve.wait_ge(xw_stored[u], 16 * b * (TILES // 2))
                    normalise(b, xin[u], xn[u]).then_inc(xn_ready[u], 1)
                for c in range(KC):
                    for h in range(HALVES):
                        m = b * KC + c
                        t = slice(h * HALF, (h + 1) * HALF)
                        seq.then(dve.tensor_scalar(inv[:, :], scale[:, c, t], 1e-10, None, ALU.max))
                        seq.then(dve.reciprocal(inv[:, :], inv[:, :]))
                        dve.wait_ge(k_ready[h], m + 1)
                        dve.wait_ge(vcopy_done[h], m + 1)
                        dve.tensor_tensor(kv[:, :], ps_k[h][:, :], v_sb[h][:, :], ALU.mult).then_inc(kv_done[h], 1)
                        dve.wait_ge(kv_done[h], m + 1)
                        seq.then(dve.tensor_tensor(kv[:, :], kv[:, :], inv[:, :], ALU.mult))
                        seq.then(dve.tensor_tensor_scan(state[:, t], ones[:, :], kv[:, :],
                                                        0.0 if h == 0 else state[:, HALF - 1:HALF],
                                                        ALU.mult, ALU.add))
                        seq.then(dve.tensor_tensor(kv[:, :], state[:, t], scale[:, c, t], ALU.mult))
                        dve.wait_ge(sig_done[h], m + 1)
                        dve.tensor_tensor(outT[:, c, t], kv[:, :], r_sb[h][:, :], ALU.mult).then_inc(out_done[h], 1)
                        dve.wait_ge(out_done[h], m + 1)
                        seq.then(dve.bn_stats(gstats[:, c * HALVES + h, :], outT[:, c, t]), apart=True)
                dve.bn_aggr(gmv[:, :], gstats[:, :, :].rearrange("p a b -> p (a b)")).then_inc(gpart_ready, 1)
                dve.wait_ge(gmean_ready, 2 * b + 1)
                dve.wait_ge(gpart_ready, 2 * b + 1)
                seq.then(dve.tensor_copy(gtmp[:, 0:1], ps_r[0][:, 0:1]))
                seq.then(dve.tensor_tensor(gtmp[:, 1:2], gmv[:, 0:1], gtmp[:, 0:1], ALU.subtract))
                dve.scalar_tensor_tensor(out=gtmp[:, 2:3], in0=gtmp[:, 1:2], scalar=gtmp[:, 1:2], in1=gmv[:, 1:2],
                                         op0=ALU.mult, op1=ALU.add).then_inc(gpart_ready, 1)
                dve.wait_ge(gmean_ready, 2 * b + 2)
                need_rstd(b, ps_r[0][:, 1:2])
                seq.then(dve.tensor_scalar(gA[:, :], gnw_sb[:, :], take_rstd(b)[:, :], None, ALU.mult))
                seq.then(dve.tensor_scalar(gB[:, :], gA[:, :], gtmp[:, 0:1], None, ALU.mult))
                seq.then(dve.tensor_tensor(gB[:, :], gnb_sb[:, :], gB[:, :], ALU.subtract))
                for c in range(KC):
                    dve.tensor_scalar(outT[:, c, :], outT[:, c, :], gA[:, c:c + 1], gB[:, c:c + 1],
                                      ALU.mult, ALU.add).then_inc(gn_applied, 1)

                def logits_of(i):
                    u, m = i % 2, b * (TILES // 2) + i // 2
                    dve.wait_ge(logit_ready[u], m + 1)
                    dve.tensor_copy(logits[:, i, 0:E], ps_l[u][:, 0:E]).then_inc(logit_copied[u], 1)

                for i in range(TILES):
                    u, m = i % 2, b * (TILES // 2) + i // 2
                    dve.wait_ge(y_ready[u], m + 1)
                    dve.wait_ge(xc_full[u], 16 * (m + 1))
                    dve.wait_ge(x2_stored[u], 16 * m)
                    dve.tensor_tensor(x2[u][:, :], ps_y[u][:, :], xin[u][:, :], ALU.add).then_inc(x2_done[u], 1)
                    dve.wait_ge(x2_done[u], m + 1)
                    row_stats(b, x2[u])
                    dve.wait_ge(xn_turned[u], (b + 1) * (TILES // 2))
                    dve.wait_ge(xw_turned[u], m)
                    dve.wait_ge(xw_stored[u], 16 * m)
                    normalise(b, x2[u], xw[u]).then_inc(xw_ready[u], 1)
                    if i >= 2:
                        logits_of(i - 2)
                logits_of(TILES - 2)
                logits_of(TILES - 1)
                for u in range(2):
                    dve.wait_ge(logit_copied[u], (b + 1) * (TILES // 2))
                dve.nop(nofuse=True)
                for i in range(TILES):
                    dve.max(top8[:, i, :], logits[:, i, 0:E]).then_inc(dve_seq, 1)
                    seq.n += 1
                dve.wait_ge(dve_seq, seq.base + seq.n)
                seq.then(dve.tensor_copy(pick8[:, :, 0:TOPK], top8[:, :, 0:TOPK]), apart=True)
                for i in range(TILES):
                    dve.match_replace(picked[:, i, :], pick8[:, i, :], logits[:, i, :], TAKEN).then_inc(dve_seq, 1)
                    seq.n += 1
                dve.wait_ge(dve_seq, seq.base + seq.n)
                dve.tensor_scalar(mask[:, :, :], picked[:, :, 0:E], TAKEN, None, ALU.is_equal).then_inc(mask_ready, 1)
                dve.wait_ge(wgt_stored, 16 * b)
                dve.tensor_tensor(wgt[:, :, :], logits[:, :, 0:E], top8[:, :, 0:1].to_broadcast([P, TILES, E]),
                                  ALU.subtract).then_inc(diff_ready, 1)
                dve.wait_ge(exp_done, b + 1)
                dve.wait_ge(mask_ready, b + 1)
                seq.then(dve.tensor_tensor(wgt[:, :, :], wgt[:, :, :], mask[:, :, :], ALU.mult))
                seq.then(dve.tensor_reduce(wsum[:, :], wgt[:, :, :], AX.X, ALU.add))
                seq.then(dve.reciprocal(wsum[:, :], wsum[:, :]))
                dve.tensor_tensor(wgt[:, :, :], wgt[:, :, :], wsum[:, :].rearrange("p (i a) -> p i a", a=1).to_broadcast([P, TILES, E]),
                                  ALU.mult).then_inc(wgt_ready, 1)
                for h in range(2):
                    dve.wait_ge(mask_turned, 2 * b + h + 1)
                    dve.scalar_tensor_tensor(out=key[:, h * HALF:(h + 1) * HALF], in0=ps_m[h][0:E, :], scalar=MEMBER,
                                             in1=ramp[:, h * HALF:(h + 1) * HALF],
                                             op0=ALU.mult, op1=ALU.add).then_inc(keys_made, 1)
                dve.wait_ge(keys_made, 2 * b + 2)
                dve.nop(nofuse=True)
                for k in range(C // 8):
                    seq.then(dve.max(cand_b[:, 8 * k:8 * k + 8], key[:, :]), apart=True)
                    if k < C // 8 - 1:
                        seq.then(dve.match_replace(key[:, :], cand_b[:, 8 * k:8 * k + 8], key[:, :], -1.0), apart=True)
                seq.then(dve.tensor_copy(cand[:, bass.ds(b * C, C)], cand_b[:, :]))

            STEPS1 = (TILES * 2 + KC * HALVES * 6 + 5 + TILES * 2 + 2 * TILES + 1 + 3 + 2 * (C // 8) - 1 + 1)
            with dve.Fori(0, SEQS) as b:
                seq.loop(b, STEPS1, before)
                phase1(b)
                assert seq.n == STEPS1, seq.n
            seq.base, seq.n = 0, before + SEQS * STEPS1

            seq.then(dve.tensor_scalar(cand[:, C:], cand[:, C:], -float(T), None, ALU.add))
            for k in range(C // 8):
                seq.then(dve.max(slots[:, 8 * k:8 * k + 8], cand[:, :]))
                if k < C // 8 - 1:
                    seq.then(dve.match_replace(cand[:, :], slots[:, 8 * k:8 * k + 8], cand[:, :], -1.0))
            seq.then(dve.tensor_scalar(bump[:, :], slots[:, :], MEMBER, MEMBER, ALU.is_ge, ALU.mult))
            seq.then(dve.tensor_tensor(slots[:, :], slots[:, :], bump[:, :], ALU.subtract))
            for h in range(2):
                dve.tensor_scalar(tok2[:, h, :], slots[:, :], -1.0, float(TOKENS), ALU.mult, ALU.add).then_inc(tok_ready, 1)
            dve.wait_ge(tok_turned, 1)
            dve.tensor_copy(idx[:, :], ps_g[0][:, 0:E]).then_inc(idx_ready, 1)
            dve.tensor_copy(pair_idx[0:C, :], chunk(ps_g[0][0:C, 0:E], 0, 2)).then_inc(idx_ready, 1)
            dve.tensor_copy(pair_idx[C:P, :], chunk(ps_g[0][C:P, 0:E], 1, 2)).then_inc(idx_ready, 1)

            with dve.Fori(0, GROUPS) as j:
                def gated(n, u):
                    dve.wait_ge(sg_ready[n], j + 1)
                    dve.wait_ge(u_ready[n], j + 1)
                    dve.wait_ge(gu_turned[n], j)
                    dve.tensor_tensor(gu[n][:, :], sg[n][:, :], ps_u[u][:, 0:I], ALU.mult).then_inc(gu_ready[n], 1)

                def turn_copy(n, src):
                    dve.wait_ge(gu_turned[n], j + 1)
                    dve.wait_ge(d_ready[n], j)
                    dve.tensor_copy(guT[n][:, :, :], src[:, 0:I].rearrange("p (c t) -> p c t", c=IC)).then_inc(guT_ready[n], 1)

                def y_odd(u):
                    dve.wait_ge(d_ready[u], j + 1)
                    dve.wait_ge(wcol_ready[u], j + 1)
                    dve.tensor_scalar(yB[u][:, :], ps_d[u][C:P, :], wcol[u][C:P, :], None, ALU.mult).then_inc(yB_ready[u], 1)

                for u in range(2):
                    dve.wait_ge(xg_full[u], 16 * (j + 1))
                    dve.wait_ge(yA_ready[u], j)
                    dve.wait_ge(yB_ready[u], j)
                    dve.tensor_copy(wcol[u][0:C, :], xg[u][0:C, bass.ds(j * 4 + (D + 2 * u), 1)])
                    dve.tensor_copy(wcol[u][C:P, :], xg[u][C:P, bass.ds(j * 4 + (D + 2 * u + 1), 1)]).then_inc(wcol_ready[u], 1)
                    gated(u, u)
                turn_copy(0, ps_ht)
                gated(2, 0)
                turn_copy(1, ps_ht)
                dve.wait_ge(added, j * ADDS)
                y_odd(0)
                turn_copy(2, ps_xt)
                y_odd(1)

        @block.tensor
        def _(pe):
            pe.wait_ge(pool_seq, 2)
            pe.wait_ge(const_ready, 2)
            pe.wait_ge(params_in, 16 * 3)

            with pe.Fori(0, SEQS) as b:
                m0 = b * (TILES // 2)
                for i in range(TILES):
                    u, m = i % 2, m0 + i // 2
                    pe.wait_ge(xn_ready[u], m + 1)
                    pe.wait_ge(xnT_ready[u], m)
                    pe.wait_ge(xwT_ready[u], m0)
                    for c in range(KC):
                        ins = pe.transpose(ps_t[u][:, c * P:(c + 1) * P], chunk(xn[u][:, :], c), ident[:, :])
                    ins.then_inc(xn_turned[u], 1)
                for c in range(KC):
                    for h in range(HALVES):
                        m = b * KC + c
                        if c == 0 and h == 0:
                            for u in range(2):
                                pe.wait_ge(xnT_ready[u], m0 + TILES // 2)
                        if c == 0:
                            pe.wait_ge(x2_done[h], m0)
                            pe.wait_ge(logit_copied[h], m0)
                            pe.wait_ge(keys_made, 2 * b)
                        for w, ps, free, ready in ((wr_sb, ps_r, sig_done, r_ready), (wv_sb, ps_v, vcopy_done, v_ready),
                                                   (wk_sb, ps_k, kv_done, k_ready)):
                            pe.wait_ge(free[h], m)
                            for k in range(KC):
                                ins = pe.matmul(ps[h][:, :], chunk(w[:, k, :], c), xnT[:, k, h * HALF:(h + 1) * HALF],
                                                start=(k == 0), stop=(k == KC - 1))
                            ins.then_inc(ready[h], 1)
                for n in range(2):
                    pe.wait_ge(gpart_ready, 2 * b + n + 1)
                    col = gmv[:, 0:1] if n == 0 else gtmp[:, 2:3]
                    if n == 0:
                        pe.wait_ge(sig_done[0], (b + 1) * KC)
                    pe.matmul(ps_r[0][:, n:n + 1], mean_mat[:, :], col, start=True, stop=True).then_inc(gmean_ready, 1)

                def project(i):
                    u, m = i % 2, m0 + i // 2
                    if i == 0:
                        pe.wait_ge(gn_applied, (b + 1) * KC)
                        pe.wait_ge(params2_in, 16 * 2)
                        pe.wait_ge(sig_done[1], (b + 1) * KC)
                    pe.wait_ge(x2_done[u], m)
                    for c in range(KC):
                        ins = pe.matmul(ps_y[u][:, :], outT[:, c, i * P:(i + 1) * P], wo_sb[:, c, :],
                                        start=(c == 0), stop=(c == KC - 1))
                    ins.then_inc(y_ready[u], 1)

                def turn(i):
                    u, m = i % 2, m0 + i // 2
                    pe.wait_ge(xw_ready[u], m + 1)
                    pe.wait_ge(xwT_ready[u], m)
                    for c in range(KC):
                        ins = pe.transpose(ps_t[u][:, c * P:(c + 1) * P], chunk(xw[u][:, :], c), ident[:, :])
                    ins.then_inc(xw_turned[u], 1)

                def route(i):
                    u, m = i % 2, m0 + i // 2
                    pe.wait_ge(xwT_ready[u], m + 1)
                    pe.wait_ge(logit_copied[u], m)
                    if i < 2:
                        pe.wait_ge(kv_done[u], (b + 1) * KC)
                    for c in range(KC):
                        ins = pe.matmul(ps_l[u][:, 0:E], xwT[u][:, c, :], router_sb[:, c, :],
                                        start=(c == 0), stop=(c == KC - 1))
                    ins.then_inc(logit_ready[u], 1)

                for i in range(TILES + 2):
                    if i < TILES:
                        project(i)
                    if 1 <= i <= TILES:
                        turn(i - 1)
                    if i >= 2:
                        route(i - 2)
                pe.wait_ge(mask_ready, b + 1)
                pe.nop(nofuse=True)
                for h in range(2):
                    pe.wait_ge(vcopy_done[h], (b + 1) * KC)
                    pe.nop(nofuse=True)
                    for i in range(TILES // 2):
                        ins = pe.transpose(ps_m[h][0:E, i * P:(i + 1) * P], mask[:, h * (TILES // 2) + i, :], ident[:, :])
                    ins.then_inc(mask_turned, 1)

            pe.wait_ge(tok_ready, 2)
            pe.transpose(ps_g[0][:, 0:E], tok2[:, :, :].rearrange("e a s -> e (a s)"), ident[0:E, 0:E]).then_inc(tok_turned, 1)
            pe.wait_ge(idx_ready, 3)
            pe.wait_ge(sh_full, 16 * 3)

            with pe.Fori(0, GROUPS) as j:
                def turn_tokens(u):
                    pe.wait_ge(xg_full[u], 16 * (j + 1))
                    if u == 0:
                        pe.wait_ge(guT_ready[2], j)
                    else:
                        pe.wait_ge(xT_ready[0], j + 1)
                    for c in range(KC):
                        ins = pe.transpose(ps_xt[:, c * P:(c + 1) * P], chunk(xg[u][:, 0:D], c), ident[:, :])
                    ins.then_inc(xg_turned[u], 1)

                def gate_and_up(u):
                    pe.wait_ge(xT_ready[u], j + 1)
                    for w, (ps, ready) in enumerate(((ps_g[u], g_ready[u]), (ps_u[u], u_ready[u]))):
                        pe.wait_ge(w_full[u][w], 32 * (j + 1))
                        last = (sg_ready, gu_ready)[w]
                        pe.wait_ge(last[2] if u == 0 else last[1], j)
                        for c in range(KC):
                            for e in range(2):
                                ins = pe.matmul(ps[e * C:(e + 1) * C, 0:I], xT[u][:, c, e * C:(e + 1) * C],
                                                gate_up(u, e, w)[:, c, :], start=(c == 0), stop=(c == KC - 1))
                        ins.then_inc(ready, 1)

                def shared_gate_and_up():
                    pe.wait_ge(xS_full, 16 * (j + 1))
                    for w, (ps, ready) in enumerate(((ps_g[0], g_ready[2]), (ps_u[0], u_ready[2]))):
                        pe.wait_ge((sg_ready, gu_ready)[w][0], j + 1)
                        for c in range(KC):
                            ins = pe.matmul(ps[:, 0:I], xS[:, c, :], sh_gu[w][:, c, :],
                                            start=(c == 0), stop=(c == KC - 1))
                        ins.then_inc(ready, 1)

                def turn_gated(n, dst):
                    pe.wait_ge(gu_ready[n], j + 1)
                    if n == 0:
                        pe.wait_ge(guT_ready[1], j)
                    elif n == 1:
                        pe.wait_ge(guT_ready[0], j + 1)
                    for c in range(IC):
                        ins = pe.transpose(dst[:, c * P:(c + 1) * P], chunk(gu[n][:, :], c, IC), ident[:, :])
                    ins.then_inc(gu_turned[n], 1)

                def down_pair(u):
                    pe.wait_ge(guT_ready[u], j + 1)
                    pe.wait_ge(w_full[u][2], 32 * (j + 1))
                    if u == 0:
                        pe.wait_ge(yS_ready, j)
                    else:
                        pe.wait_ge(yA_ready[1], j)
                        pe.wait_ge(yB_ready[1], j)
                    for c in range(IC):
                        for e in range(2):
                            ins = pe.matmul(ps_d[u][e * C:(e + 1) * C, :], guT[u][:, c, e * C:(e + 1) * C],
                                            down(u, e)[:, c, :], start=(c == 0), stop=(c == IC - 1))
                    ins.then_inc(d_ready[u], 1)

                def down_shared():
                    pe.wait_ge(guT_ready[2], j + 1)
                    pe.wait_ge(yA_ready[0], j + 1)
                    pe.wait_ge(yB_ready[0], j + 1)
                    for c in range(IC):
                        ins = pe.matmul(ps_d[0][:, :], guT[2][:, c, :], sh_dn[:, c, :],
                                        start=(c == 0), stop=(c == IC - 1))
                    ins.then_inc(d_ready[2], 1)

                turn_tokens(0)
                gate_and_up(0)
                turn_tokens(1)
                gate_and_up(1)
                turn_gated(0, ps_ht)
                shared_gate_and_up()
                down_pair(0)
                turn_gated(1, ps_ht)
                turn_gated(2, ps_xt)
                down_pair(1)
                down_shared()


_ARGS = ["L0_attn_x", "L0_attn_Wr", "L0_attn_Wk", "L0_attn_Wv", "L0_attn_Wo", "L0_attn_decay", "L0_attn_gn_weight",
         "L0_attn_gn_bias", "L0_ffn_w_router", "L0_ffn_w_gate", "L0_ffn_w_up", "L0_ffn_w_down",
         "L0_ffn_w_sh_gate", "L0_ffn_w_sh_up", "L0_ffn_w_sh_down"]
_SWAPPED = {"L0_attn_Wr", "L0_attn_Wk", "L0_attn_Wv", "L0_attn_Wo", "L0_ffn_w_router"}


def kernel(**inputs):
    import numpy as _np
    import concourse.bacc as _bacc
    from concourse import mybir as _mybir
    from concourse.bass_utils import run_bass_kernel_spmd as _run

    nc = _bacc.Bacc("TRN2", target_bir_lowering=False, num_devices=1)
    arrays, args = {}, []
    for name in _ARGS:
        a = _np.asarray(inputs[name])
        if name in _SWAPPED:
            a = a.T
        if name == "L0_attn_x":
            a = a.reshape(-1, a.shape[-1])
        a = _np.ascontiguousarray(a)
        arrays[f"in_{name}"] = a
        args.append(nc.dram_tensor(f"in_{name}", a.shape, _mybir.dt.from_np(a.dtype), kind="ExternalInput").ap())
    shape = inputs["L0_attn_x"].shape
    out = nc.dram_tensor("out_dram", (shape[0] * shape[1], shape[2]), F32, kind="ExternalOutput").ap()
    moe_block(nc, *args, out)
    r = _run(nc, [arrays], core_ids=[0])
    return r.results[0]["out_dram"].reshape(shape)
```

```python
from contextlib import ExitStack

import concourse.bass as bass
from concourse import mybir

F32 = mybir.dt.float32
F32R = mybir.dt.float32r
U32 = mybir.dt.uint32
I32 = mybir.dt.int32
ALU = mybir.AluOpType
ACT = mybir.ActivationFunctionType
AX = mybir.AxisListType

P = 128
SEQS, T, D = 2, 1024, 512
TOKENS = SEQS * T
KC = D // P
TILES = T // P
HALF = 512
STEPS = KC * T // HALF
E, TOPK, I, C = 64, 4, 384, 64
IC = I // P
ROW = D + E
LN_EPS = 1e-5
SENTINEL, TAKEN = -3.0e38, -3.3e38
NORMS = 2 * TILES + 1
MEMBER = 4096.0
GROUPS = E // 4
W = KC * I
PIECES = 2
ADD = 16
ADDS = 5 * ADD


def moe_block(nc, x, wr, wk, wv, wo, decay, gn_w, gn_b, w_router, w_gate, w_up, w_down,
              sh_gate, sh_up, sh_down, out):
    xw_dram = nc.dram_tensor("xw_dram", [TOKENS, ROW], F32, kind="Internal").ap()
    xt_dram = nc.dram_tensor("xt_dram", [TOKENS // P, P, D], F32, kind="Internal").ap()

    with ExitStack() as ctx:
        def sem(name):
            return ctx.enter_context(nc.semaphore(name))

        def sem2(name):
            return [sem(f"{name}{u}") for u in range(2)]

        bank = [ctx.enter_context(nc.psum_tensor(f"bank{i}", [P, 512], F32)) for i in range(8)]
        ps_r, ps_k, ps_v, ps_t = bank[0:2], bank[2:4], bank[4:6], bank[6:8]
        ps_y, ps_l = ps_r, ps_k
        ps_g, ps_u, ps_xt, ps_ht, ps_d = bank[0:2], bank[2:4], bank[4], bank[5], bank[6:8]

        start = (nc.sbuf_base + 63) // 64 * 64
        top = [start]

        def room(size):
            at = top[0]
            top[0] += size
            return at

        def tile(name, shape, dt=F32, at=None):
            size = 4
            for n in shape[1:]:
                size *= n
            return nc.alloc_sbuf_tensor_at(name, shape, dt, offset=room((size + 31) // 32 * 32) if at is None else at)

        K4 = 4 * T
        ident = tile("ident", [P, P])
        mean_mat = tile("mean_mat", [P, P])
        ones = tile("ones", [P, 1])
        minus_half = tile("minus_half", [P, 1])
        dec = tile("dec", [P, 4, KC])
        gnw_sb, gnb_sb = tile("gnw_sb", [P, KC]), tile("gnb_sb", [P, KC])
        ramp = tile("ramp", [E, T])
        wo_sb = tile("wo_sb", [P, KC, D])
        router_sb = tile("router_sb", [P, KC, E])
        w_at = [room(2 * 3 * W * 4) for _ in range(2)]
        w_sb = [tile(f"w_sb{u}", [P, 2, 3, W], at=w_at[u]) for u in range(2)]
        lo_at = [w_at[1] + n * 2 * K4 for n in range(3)]
        w_lo = [tile(f"{n}_lo", [P, KC, D], F32R, at=lo_at[i]) for i, n in enumerate(("wr", "wv", "wk"))]
        x3_at = room(K4)
        x_lo = [tile(f"x_lo{k}", [P, T], F32R, at=(w_at[1] + 6 * K4 + k * K4) if k < 3 else x3_at) for k in range(KC)]
        hi_at = room(6 * K4)
        w_hi = [tile(f"{n}_hi", [P, KC, D], F32R, at=hi_at + i * 2 * K4) for i, n in enumerate(("wr", "wv", "wk"))]
        xhi_at = room(4 * K4)
        x_hi = tile("x_hi", [P, KC, T], F32R, at=xhi_at)
        scale_at, inv_at, out_at = room(4 * K4), room(4 * K4), room(4 * K4)
        scale, inv, outT = (tile(n, [P, KC, T], at=a) for n, a in (("scale", scale_at), ("inv", inv_at), ("outT", out_at)))
        rx_at, vx_at, st_at = room(K4), room(K4), room(K4)
        r_sb = [tile(f"r_sb{h}", [P, HALF], at=rx_at + h * 2048) for h in range(2)]
        v_sb = [tile(f"v_sb{h}", [P, HALF], at=vx_at + h * 2048) for h in range(2)]
        state = tile("state", [P, T], at=st_at)
        xwT = [tile(f"xwT{u}", [P, KC, P], at=rx_at + u * 2048) for u in range(2)]
        x2 = [tile(f"x2_{u}", [P, D], at=vx_at + u * 2048) for u in range(2)]
        xc = [tile(f"xc{u}", [P, D], at=st_at + u * 2048) for u in range(2)]
        raw = [tile(f"{n}_raw", [P, KC, D], at=a) for n, a in (("wr", out_at), ("wv", out_at + 2 * K4), ("wk", rx_at))]
        pos_i = tile("pos_i", [P, T], I32, at=st_at)
        xin_at, xn_at, xw_at = room(K4), room(K4), room(K4)
        xin = [tile(f"xin{u}", [P, D], at=xin_at + u * 2048) for u in range(2)]
        xn = [tile(f"xn{u}", [P, D], at=xn_at + u * 2048) for u in range(2)]
        xw = [tile(f"xw{u}", [P, D], at=xw_at + u * 2048) for u in range(2)]
        kv = tile("kv", [P, HALF], at=xw_at)
        stats = tile("stats", [P, 6])
        mv = [tile(f"mv{u}", [P, 2]) for u in range(2)]
        var_eps = [tile(f"var_eps{u}", [P, 1]) for u in range(2)]
        rstd = [tile(f"rstd{u}", [P, 1]) for u in range(2)]
        gstats = tile("gstats", [P, STEPS, 6])
        gmv = tile("gmv", [P, 2])
        gtmp = tile("gtmp", [P, 4])
        gA, gB = tile("gA", [P, KC]), tile("gB", [P, KC])
        logits = tile("logits", [P, TILES, E + 4])
        top8 = tile("top8", [P, TILES, 8])
        pick8 = tile("pick8", [P, TILES, 8])
        mask = tile("mask", [P, TILES, E], at=xn_at)
        wgt = tile("wgt", [P, TILES, E], at=xn_at + 2048)
        wsum = tile("wsum", [P, TILES, 1])
        key = tile("key", [E, T], at=xin_at)
        cand = tile("cand", [E, SEQS * C])
        slots = tile("slots", [E, C], at=x3_at)
        bump = tile("bump", [E, C], at=x3_at + 256)
        tok2 = tile("tok2", [E, 2, C], at=x3_at + 512)
        idx = tile("idx", [P, E], U32)
        pair_idx = tile("pair_idx", [P, E // 2], U32)
        gidx = [tile(f"gidx{u}", [P, 1], U32) for u in range(2)]
        sidx = [tile(f"sidx{u}", [C, 1], U32) for u in range(2)]
        wcol = [tile(f"wcol{u}", [P, 1]) for u in range(2)]
        arena_end = top[0]

        top[0] = scale_at
        xT = [tile(f"xT{u}", [P, KC, P]) for u in range(2)]
        xS = tile("xS", [P, KC, P])
        sg = [tile(f"sg{n}", [P, I]) for n in range(3)]
        gu = [tile(f"gu{n}", [P, I]) for n in range(3)]
        guT = [tile(f"guT{n}", [P, IC, P]) for n in range(3)]
        yA = [tile(f"yA{u}", [C, D]) for u in range(2)]
        yB = [tile(f"yB{u}", [C, D]) for u in range(2)]
        assert top[0] <= out_at
        top[0] = xhi_at
        yS = tile("yS", [P, D])
        xg = [tile(f"xg{u}", [P, ROW]) for u in range(2)]
        assert top[0] <= scale_at
        sh_sb = tile("sh_sb", [P, 3, W], at=hi_at)
        ctx.enter_context(nc.sbuf_tensor("arena", [P, (arena_end - nc.sbuf_base + 3) // 4], F32))

        def gate_up(u, e, which):
            return w_sb[u][:, e, which, :].rearrange("p (c n) -> p c n", c=KC)

        def down(u, e):
            return w_sb[u][:, e, 2, :].rearrange("p (c n) -> p c n", c=IC)

        sh_gu = [sh_sb[:, w, :].rearrange("p (c n) -> p c n", c=KC) for w in range(2)]
        sh_dn = sh_sb[:, 2, :].rearrange("p (c n) -> p c n", c=IC)

        def chunk(ap, c, n=KC):
            return ap.rearrange("p (m c) -> p c m", c=n)[:, c, :]

        def need(eng, s, v):
            if not isinstance(v, int) or v > 0:
                eng.wait_ge(s, v)

        vectors_in = sem("vectors_in")
        raw_in = [sem(f"raw_in{i}") for i in range(3)]
        params_in = sem("params_in")
        sh_full = sem("sh_full")
        ident_steps = sem("ident_steps")
        const_ready = sem("const_ready")
        setup = sem("setup")
        hi_ready, lo_ready = sem("hi_ready"), sem("lo_ready")
        xin_full, xc_full = sem2("xin_full"), sem2("xc_full")
        var_ready, rstd_ready = sem("var_ready"), sem("rstd_ready")
        xn_ready = sem("xn_ready")
        xn_turned = sem("xn_turned")
        xhi_ready, xlo_ready = sem("xhi_ready"), sem("xlo_ready")
        inv_ready = sem("inv_ready")
        r_ready, k_ready, v_ready = sem("r_ready"), sem("k_ready"), sem("v_ready")
        sig_done, vcopy_done = sem("sig_done"), sem("vcopy_done")
        rscaled, vscaled = sem("rscaled"), sem("vscaled")
        kv_done, out_done = sem("kv_done"), sem("out_done")
        dve_seq = sem("dve_seq")
        pool_seq = sem("pool_seq")
        gpart_ready = sem("gpart_ready")
        gmean_ready = sem("gmean_ready")
        gn_applied = sem("gn_applied")
        y_ready = sem("y_ready")
        x2_done, xw_ready = sem("x2_done"), sem("xw_ready")
        xw_turned, xwT_ready = sem("xw_turned"), sem("xwT_ready")
        logit_ready, logit_copied = sem("logit_ready"), sem("logit_copied")
        x2_stored, xw_stored, xwT_stored = sem2("x2_stored"), sem2("xw_stored"), sem2("xwT_stored")
        mask_ready, diff_ready, wgt_ready = sem("mask_ready"), sem("diff_ready"), sem("wgt_ready")
        exp_done = sem("exp_done")
        wgt_stored = sem("wgt_stored")
        mask_turned, keys_made = sem("mask_turned"), sem("keys_made")
        tok_ready, tok_turned, idx_ready = sem("tok_ready"), sem("tok_turned"), sem("idx_ready")
        w_full = [sem(f"w_full{n}") for n in range(2 * PIECES)]
        xg_full, xg_turned, xT_ready, wcol_ready = sem2("xg_full"), sem2("xg_turned"), sem2("xT_ready"), sem2("wcol_ready")
        xS_full = sem("xS_full")
        g_ready, u_ready, sg_ready, gu_ready, gu_turned, guT_ready, d_ready = (
            [sem(f"{n}{u}") for u in range(3)]
            for n in ("g_ready", "u_ready", "sg_ready", "gu_ready", "gu_turned", "guT_ready", "d_ready"))
        yA_ready, yB_ready, yS_ready = sem2("yA_ready"), sem2("yB_ready"), sem("yS_ready")
        added = sem("added")

        class Steps:

            def __init__(self, eng, s):
                self.eng, self.s, self.base, self.n = eng, s, 0, 0

            def then(self, ins, apart=False):
                self.n += 1
                ins.then_inc(self.s, 1)
                self.eng.wait_ge(self.s, self.base + self.n)
                if apart:
                    self.eng.nop(nofuse=True)

            def loop(self, i, per, before):
                self.base, self.n = i * per + before, 0

        def groups(eng, body):
            body(0)
            with eng.Fori(1, GROUPS) as j:
                body(j)

        block = ctx.enter_context(nc.Block())

        @block.sync
        def _(sp):
            def load_x(n, full, dst, read):
                need(sp, read, n - 1)
                sp.dma_start(dst[n % 2][:, :], x[n * P:(n + 1) * P, :]).then_inc(full[n % 2], 16)

            def wait(s, v):
                need(sp, s, v)
                if not isinstance(v, int):
                    sp.nop(nofuse=True)

            def load_matrix(j, u, k):
                wait((g_ready[u], u_ready[u], d_ready[u])[k], j)
                m = j * 6 + (u * 3 + k)
                for n in range(2 * PIECES):
                    e, h = n // PIECES, n % PIECES
                    if n < 2 * PIECES - 1:
                        wait(w_full[n + 1], m * 16)
                    else:
                        wait(w_full[0], m * 16 + 16)
                    cols = slice(h * W // PIECES, (h + 1) * W // PIECES)
                    src = (w_gate, w_up, w_down)[k][bass.ds(j * 4 + (u * 2 + e), 1)].rearrange("a (p c) n -> (a p) (c n)", p=P)
                    sp.dma_start(w_sb[u][:, e, k, cols], src[:, cols]).then_inc(w_full[n], 16)

            def load_shared_tile(j):
                wait(u_ready[2], j)
                sp.dma_start(xS[:, :, :].rearrange("p c t -> p (c t)"),
                             xt_dram[bass.ds(j, 1)].rearrange("a p n -> (a p) n")).then_inc(xS_full, 16)

            for n in range(2):
                load_x(n, xin_full, xin, xn_ready)
            sp.dma_start(dec[:, 0, :], decay.rearrange("(p c) -> p c", c=KC)).then_inc(vectors_in, 16)
            for i, w in enumerate((wr, wv, wk)):
                sp.dma_start(raw[i][:, :, :], w.rearrange("(p c) n -> p c n", c=KC)).then_inc(raw_in[i], 16)
            sp.dma_start(gnw_sb[:, :], gn_w.rearrange("(p c) -> p c", c=KC)).then_inc(vectors_in, 16)
            sp.dma_start(gnb_sb[:, :], gn_b.rearrange("(p c) -> p c", c=KC)).then_inc(vectors_in, 16)
            for n in range(2, TILES + 2):
                load_x(n, xin_full, xin, xn_ready)
            for k in range(3):
                load_matrix(0, 0, k)
            sp.wait_ge(out_done, STEPS)
            for n in range(TILES):
                load_x(n, xc_full, xc, x2_done)
                if n + TILES + 2 < 2 * TILES:
                    load_x(n + TILES + 2, xin_full, xin, xn_ready)
            sp.wait_ge(k_ready, 2 * STEPS)
            sp.wait_ge(out_done, 2 * STEPS)
            for n in range(TILES, TILES + 2):
                load_x(n, xc_full, xc, x2_done)
            for k, w in enumerate((sh_gate, sh_up, sh_down)):
                load_matrix(0, 1, k)
                load_x(TILES + 2 + 2 * k, xc_full, xc, x2_done)
                sp.dma_start(sh_sb[:, k, :], w.rearrange("(p c) n -> p (c n)", p=P)).then_inc(sh_full, 16)
                load_x(TILES + 3 + 2 * k, xc_full, xc, x2_done)
            for u in range(2):
                sp.wait_ge(xwT_stored[u], 16 * SEQS * TILES // 2)
            load_shared_tile(0)
            with sp.Fori(1, GROUPS) as j:
                for k in range(3):
                    load_matrix(j, 0, k)
                load_shared_tile(j)
                for k in range(3):
                    load_matrix(j, 1, k)

        @block.gpsimd
        def _(pool):
            seq = Steps(pool, pool_seq)
            pool.iota(pos_i[:, :], pattern=[[1, T]], base=0, channel_multiplier=0).then_inc(const_ready, 1)
            pool.memset(minus_half[:, :], -0.5)
            pool.memset(ident[:, :], 0.0).then_inc(ident_steps, 1)
            pool.wait_ge(ident_steps, 1)
            pool.affine_select(out=ident[:, :], in_=ident[:, :], compare_op=ALU.not_equal, fill=1.0,
                               base=0, pattern=[[-1, P]], channel_multiplier=1).then_inc(ident_steps, 1)
            norms = [0]

            def powers(count):
                for _ in range(count):
                    n = norms[0]
                    pool.wait_ge(var_ready, n + 1)
                    pool.tensor_tensor(rstd[n % 2][:, :], var_eps[n % 2][:, :], minus_half[:, :],
                                       ALU.pow).then_inc(rstd_ready, 1)
                    norms[0] += 1

            powers(2)
            pool.memset(mean_mat[:, :], 1.0 / P)
            pool.memset(ones[:, :], 1.0)
            pool.memset(logits[:, :, E:], SENTINEL)
            pool.memset(pick8[:, :, TOPK:], SENTINEL).then_inc(const_ready, 1)
            for i in range(3):
                powers(2)
                pool.wait_ge(hi_ready, i + 1)
                pool.tensor_tensor(w_lo[i][:, :, :], raw[i][:, :, :], w_hi[i][:, :, :].bitcast(F32),
                                   ALU.subtract).then_inc(lo_ready, 1)
            pool.iota(ramp[:, :], pattern=[[-1, T]], base=TOKENS, channel_multiplier=0,
                      allow_small_or_imprecise_dtypes=True).then_inc(const_ready, 1)
            pool.dma_start(wo_sb[:, :, :], wo.rearrange("(p c) n -> p c n", c=KC)).then_inc(params_in, 16)
            pool.dma_start(router_sb[:, :, :], w_router.rearrange("(p c) n -> p c n", c=KC)).then_inc(params_in, 16)

            def scale_step(s):
                h, b, c = s % 2, s // STEPS, s % STEPS // 2
                t = slice(h * HALF, (h + 1) * HALF)
                pool.wait_ge(vcopy_done, s + 1)
                if b == 0:
                    pool.wait_ge(inv_ready, s + 1)
                pool.tensor_tensor(v_sb[h][:, :], v_sb[h][:, :], inv[:, c, t], ALU.mult).then_inc(vscaled, 1)
                pool.wait_ge(sig_done, s + 1)
                pool.tensor_tensor(r_sb[h][:, :], r_sb[h][:, :], scale[:, c, t], ALU.mult).then_inc(rscaled, 1)

            def store_tile(n):
                rows = slice(n * P, (n + 1) * P)
                pool.wait_ge(x2_done, n + 1)
                pool.dma_start(out[rows, :], x2[n % 2][:, :]).then_inc(x2_stored[n % 2], 16)
                pool.wait_ge(xw_ready, n + 1)
                pool.dma_start(xw_dram[rows, 0:D], xw[n % 2][:, :]).then_inc(xw_stored[n % 2], 16)

            def store_turned(n):
                pool.wait_ge(xwT_ready, n + 1)
                pool.dma_start(xt_dram[n], xwT[n % 2][:, :, :].rearrange("p c t -> p (c t)")).then_inc(xwT_stored[n % 2], 16)

            def store_weights(b):
                pool.wait_ge(wgt_ready, b + 1)
                pool.dma_start(xw_dram[b * T:(b + 1) * T, D:ROW].rearrange("(i p) e -> p i e", p=P),
                               wgt[:, :, :]).then_inc(wgt_stored, 16)

            for s in range(STEPS):
                scale_step(s)
            powers(2)
            for i in range(TILES):
                if i + 1 < TILES:
                    powers(1)
                powers(1)
                if i:
                    store_turned(i - 1)
                store_tile(i)
            store_turned(TILES - 1)
            for s in range(STEPS, 2 * STEPS):
                scale_step(s)
                if s == STEPS + 4:
                    store_weights(0)
            powers(1)
            for n in range(TILES, 2 * TILES):
                powers(1)
                if n > TILES:
                    store_turned(n - 1)
                store_tile(n)
            store_turned(2 * TILES - 1)
            store_weights(1)

            def gather(j, u):
                need(pool, xg_turned[u], j)
                need(pool, wcol_ready[u], j)
                seq.then(pool.tensor_copy(gidx[u][:, :], pair_idx[:, bass.ds(j * 2 + u, 1)]), apart=True)
                pool.indirect_dma_start(out=xg[u][:, :], out_offset=None, in_=xw_dram[:, :],
                                        in_offset=bass.IndirectOffsetOnAxis(ap=gidx[u][:, :], axis=0),
                                        ).then_inc(xg_full[u], 16)

            def add_group(j):
                n = 0
                for u in range(2):
                    for e, (y, ready) in enumerate(((yA, yA_ready), (yB, yB_ready))):
                        pool.wait_ge(ready[u], j + 1)
                        seq.then(pool.tensor_copy(sidx[e][:, :], idx[0:C, bass.ds(j * 4 + u * 2 + e, 1)]), apart=True)
                        need(pool, added, j * ADDS + n * ADD)
                        pool.nop(nofuse=True)
                        pool.indirect_dma_start(out=out[:, :],
                                                out_offset=bass.IndirectOffsetOnAxis(ap=sidx[e][:, :], axis=0),
                                                in_=y[u][:, :], in_offset=None,
                                                compute_op=ALU.add).then_inc(added, ADD)
                        n += 1
                pool.wait_ge(yS_ready, j + 1)
                pool.wait_ge(added, j * ADDS + n * ADD)
                pool.dma_start(out[bass.ds(j * P, P), :], yS[:, :], accum_op=ALU.add).then_inc(added, ADD)

            for u in range(2):
                pool.wait_ge(x2_stored[u], 16 * TILES)
                pool.wait_ge(xw_stored[u], 16 * TILES)
            pool.wait_ge(wgt_stored, 16 * SEQS)
            pool.wait_ge(idx_ready, 3)
            for u in range(2):
                gather(0, u)
            for u in range(2):
                gather(1, u)
            add_group(0)
            before = seq.n
            with pool.Fori(1, GROUPS - 1) as j:
                seq.loop(j - 1, 6, before)
                for u in range(2):
                    gather(j + 1, u)
                add_group(j)
            seq.base, seq.n = 0, before + 6 * (GROUPS - 2)
            add_group(GROUPS - 1)
            pool.wait_ge(added, GROUPS * ADDS)

        @block.scalar
        def _(act):
            def turned_x(n):
                bank_n = n % 2 if n < TILES else 1
                act.wait_ge(xn_turned, n + 1)
                if n == TILES:
                    act.wait_ge(k_ready, STEPS)
                i = n % TILES
                act.activation(x_hi[:, :, i * P:(i + 1) * P], ps_t[bank_n][:, :].rearrange("p (c t) -> p c t", c=KC),
                               ACT.Copy).then_inc(xhi_ready, 1)

            def step(s):
                h = s % 2
                act.wait_ge(r_ready, s + 1)
                need(act, out_done, s - 1)
                if s == 0:
                    act.wait_ge(lo_ready, 3)
                if s == STEPS:
                    act.wait_ge(logit_ready, TILES)
                    for u in range(2):
                        act.wait_ge(xwT_stored[u], 16 * TILES // 2)
                act.activation(r_sb[h][:, :], ps_r[h][:, :], ACT.Sigmoid).then_inc(sig_done, 1)
                act.wait_ge(v_ready, s + 1)
                need(act, kv_done, s - 1)
                if s == STEPS:
                    act.wait_ge(xw_ready, TILES)
                    for u in range(2):
                        act.wait_ge(x2_stored[u], 16 * TILES // 2)
                act.activation(v_sb[h][:, :], ps_v[h][:, :], ACT.Copy).then_inc(vcopy_done, 1)

            def turned_xw(n):
                b = n // TILES
                bank_n = n % 2 if b else 0
                act.wait_ge(xw_turned, n + 1)
                if n % TILES < 2:
                    act.wait_ge(out_done, (b + 1) * STEPS)
                need(act, logit_ready, n - 1)
                need(act, xwT_stored[n % 2], 16 * (n // 2))
                act.activation(xwT[n % 2][:, :, :], ps_t[bank_n][:, :].rearrange("p (c t) -> p c t", c=KC),
                               ACT.Copy).then_inc(xwT_ready, 1)

            def exponentials(b):
                act.wait_ge(diff_ready, b + 1)
                act.activation(wgt[:, :, :], wgt[:, :, :], ACT.Exp).then_inc(exp_done, 1)

            act.wait_ge(vectors_in, 16 * 3)
            act.activation(dec[:, 1, :], dec[:, 0, :], ACT.Sigmoid).then_inc(setup, 1)
            act.wait_ge(setup, 2)
            act.activation(dec[:, 3, :], dec[:, 2, :], ACT.Ln).then_inc(setup, 1)
            act.wait_ge(setup, 3)
            act.wait_ge(const_ready, 1)
            for c in range(KC):
                act.activation(scale[:, c, :], pos_i[:, :], ACT.Exp, scale=dec[:, 3, c:c + 1]).then_inc(setup, 1)
            for n in range(TILES):
                turned_x(n)
                if n % 2 == 0 and n < 6:
                    act.wait_ge(raw_in[n // 2], 16)
                    act.activation(w_hi[n // 2][:, :, :], raw[n // 2][:, :, :], ACT.Copy).then_inc(hi_ready, 1)
            for s in range(STEPS):
                step(s)
            turned_x(TILES)
            for i in range(TILES + 1):
                if i + 1 < TILES:
                    turned_x(TILES + 1 + i)
                if i:
                    turned_xw(i - 1)
            for s in range(STEPS, 2 * STEPS):
                step(s)
                if s == STEPS + 1:
                    exponentials(0)
            for n in range(TILES, 2 * TILES):
                turned_xw(n)
            exponentials(1)

            def group(j):
                def silu(n, u):
                    act.wait_ge(g_ready[n], j + 1)
                    need(act, gu_ready[n], j)
                    act.activation(sg[n][:, :], ps_g[u][:, 0:I], ACT.Silu).then_inc(sg_ready[n], 1)

                for u in range(2):
                    act.wait_ge(xg_turned[u], j + 1)
                    need(act, u_ready[u], j)
                    act.activation(xT[u][:, :, :], ps_xt[:, :].rearrange("p (c t) -> p c t", c=KC),
                                   ACT.Copy).then_inc(xT_ready[u], 1)
                    silu(u, u)
                silu(2, 0)
                for u in range(2):
                    act.wait_ge(d_ready[u], j + 1)
                    act.wait_ge(wcol_ready[u], j + 1)
                    need(act, added, (j - 1) * ADDS + (2 * u + 1) * ADD)
                    act.activation(yA[u][:, :], ps_d[u][0:C, :], ACT.Copy, scale=wcol[u][0:C, :]).then_inc(yA_ready[u], 1)
                act.wait_ge(d_ready[2], j + 1)
                need(act, added, (j - 1) * ADDS + ADDS)
                act.activation(yS[:, :], ps_d[0][:, :], ACT.Copy).then_inc(yS_ready, 1)

            groups(act, group)

        @block.vector
        def _(dve):
            seq = Steps(dve, dve_seq)
            norms = [0, 0]

            def give_variance(var):
                dve.tensor_scalar(var_eps[norms[0] % 2][:, :], var, LN_EPS, None, ALU.add).then_inc(var_ready, 1)
                norms[0] += 1

            def take_power():
                norms[1] += 1
                dve.wait_ge(rstd_ready, norms[1])
                return rstd[(norms[1] - 1) % 2]

            def row_stats(src):
                u = norms[0] % 2
                seq.then(dve.bn_stats(stats[:, :], src[:, :]))
                seq.then(dve.bn_aggr(mv[u][:, :], stats[:, :]))
                give_variance(mv[u][:, 1:2])

            def normalise(src, dst):
                u = norms[1] % 2
                r = take_power()
                return dve.tensor_scalar(dst[:, :], src[:, :], mv[u][:, 0:1], r[:, :], ALU.subtract, ALU.mult)

            def x_stats(n):
                dve.wait_ge(xin_full[n % 2], 16 * (n // 2 + 1))
                row_stats(xin[n % 2])

            def x_norm(n):
                need(dve, xn_turned, n - 1)
                normalise(xin[n % 2], xn[n % 2]).then_inc(xn_ready, 1)

            def x_low(n):
                bank_n = n % 2 if n < TILES else 1
                i = n % TILES
                dve.wait_ge(xhi_ready, n + 1)
                for k in range(KC):
                    t = slice(i * P, (i + 1) * P)
                    ins = dve.tensor_tensor(x_lo[k][:, t], ps_t[bank_n][:, k * P:(k + 1) * P],
                                            x_hi[:, k, t].bitcast(F32), ALU.subtract)
                ins.then_inc(xlo_ready, 1)

            def invert(s):
                c, h = s // 2, s % 2
                t = slice(h * HALF, (h + 1) * HALF)
                seq.then(dve.tensor_scalar(inv[:, c, t], scale[:, c, t], 1e-10, None, ALU.max))
                dve.reciprocal(inv[:, c, t], inv[:, c, t]).then_inc(inv_ready, 1)

            def step(s):
                h, c = s % 2, s % STEPS // 2
                t = slice(h * HALF, (h + 1) * HALF)
                dve.wait_ge(k_ready, s + 1)
                dve.wait_ge(vscaled, s + 1)
                if s == STEPS:
                    dve.wait_ge(xw_turned, TILES)
                    dve.wait_ge(xw_stored[0], 16 * TILES // 2)
                dve.tensor_tensor(kv[:, :], ps_k[h][:, :], v_sb[h][:, :], ALU.mult).then_inc(kv_done, 1)
                dve.wait_ge(kv_done, s + 1)
                seq.then(dve.tensor_tensor_scan(state[:, t], ones[:, :].to_broadcast([P, HALF]), kv[:, :],
                                                0.0 if h == 0 else state[:, HALF - 1:HALF], ALU.mult, ALU.add))
                dve.wait_ge(rscaled, s + 1)
                dve.tensor_tensor(outT[:, c, t], state[:, t], r_sb[h][:, :], ALU.mult).then_inc(out_done, 1)
                dve.wait_ge(out_done, s + 1)
                seq.then(dve.bn_stats(gstats[:, s % STEPS, :], outT[:, c, t]), apart=True)

            def partition_mean():
                dve.bn_aggr(gmv[:, :], gstats[:, :, :].rearrange("p a b -> p (a b)")).then_inc(gpart_ready, 1)

            def partition_variance(b):
                dve.wait_ge(gmean_ready, 2 * b + 1)
                dve.wait_ge(gpart_ready, 2 * b + 1)
                seq.then(dve.tensor_copy(gtmp[:, 0:1], ps_r[0][:, 0:1]))
                seq.then(dve.tensor_tensor(gtmp[:, 1:2], gmv[:, 0:1], gtmp[:, 0:1], ALU.subtract))
                dve.scalar_tensor_tensor(out=gtmp[:, 2:3], in0=gtmp[:, 1:2], scalar=gtmp[:, 1:2], in1=gmv[:, 1:2],
                                         op0=ALU.mult, op1=ALU.add).then_inc(gpart_ready, 1)

            def sequence_variance(b):
                dve.wait_ge(gmean_ready, 2 * b + 2)
                give_variance(ps_r[0][:, 1:2])

            def apply_sequence_norm():
                r = take_power()
                seq.then(dve.tensor_scalar(gA[:, :], gnw_sb[:, :], r[:, :], None, ALU.mult))
                seq.then(dve.tensor_scalar(gB[:, :], gA[:, :], gtmp[:, 0:1], None, ALU.mult))
                seq.then(dve.tensor_tensor(gB[:, :], gnb_sb[:, :], gB[:, :], ALU.subtract))
                for h in range(2):
                    t = slice(h * HALF, (h + 1) * HALF)
                    for c in range(KC):
                        dve.tensor_scalar(outT[:, c, t], outT[:, c, t], gA[:, c:c + 1], gB[:, c:c + 1],
                                          ALU.mult, ALU.add).then_inc(gn_applied, 1)

            def residual(n):
                u = n % 2
                dve.wait_ge(y_ready, n + 1)
                dve.wait_ge(xc_full[u], 16 * (n // 2 + 1))
                need(dve, x2_stored[u], 16 * (n // 2))
                dve.tensor_tensor(x2[u][:, :], ps_y[u][:, :], xc[u][:, :], ALU.add).then_inc(x2_done, 1)
                dve.wait_ge(x2_done, n + 1)
                row_stats(x2[u])

            def second_norm(n):
                u = n % 2
                need(dve, xw_turned, n - 1)
                need(dve, xw_stored[u], 16 * (n // 2))
                normalise(x2[u], xw[u]).then_inc(xw_ready, 1)

            def take_logits(n):
                dve.wait_ge(logit_ready, n + 1)
                dve.tensor_copy(logits[:, n % TILES, 0:E], ps_l[n % 2][:, 0:E]).then_inc(logit_copied, 1)

            def route(b):
                dve.wait_ge(logit_copied, (b + 1) * TILES)
                for i in range(TILES):
                    dve.max(top8[:, i, :], logits[:, i, 0:E]).then_inc(dve_seq, 1)
                    seq.n += 1
                dve.wait_ge(dve_seq, seq.n)
                seq.then(dve.tensor_copy(pick8[:, :, 0:TOPK], top8[:, :, 0:TOPK]))
                dve.wait_ge(xn_turned, 2 * TILES)
                need(dve, wgt_stored, 16 * b)
                dve.tensor_tensor(wgt[:, :, :], logits[:, :, 0:E], top8[:, :, 0:1].to_broadcast([P, TILES, E]),
                                  ALU.subtract).then_inc(diff_ready, 1)
                dve.wait_ge(diff_ready, b + 1)
                for i in range(TILES):
                    dve.match_replace(logits[:, i, :], pick8[:, i, :], logits[:, i, :], TAKEN).then_inc(dve_seq, 1)
                    seq.n += 1
                dve.wait_ge(dve_seq, seq.n)
                dve.tensor_scalar(mask[:, :, :], logits[:, :, 0:E], TAKEN, None, ALU.is_equal).then_inc(mask_ready, 1)
                seq.then(dve.memset(logits[:, :, E:], SENTINEL))
                yield
                for h in range(2):
                    dve.wait_ge(mask_turned, 2 * b + h + 1)
                    dve.scalar_tensor_tensor(out=key[:, h * HALF:(h + 1) * HALF], in0=ps_t[h][0:E, :], scalar=MEMBER,
                                             in1=ramp[:, h * HALF:(h + 1) * HALF],
                                             op0=ALU.mult, op1=ALU.add).then_inc(keys_made, 1)
                dve.wait_ge(exp_done, b + 1)
                dve.wait_ge(mask_ready, b + 1)
                seq.then(dve.tensor_tensor(wgt[:, :, :], wgt[:, :, :], mask[:, :, :], ALU.mult))
                seq.then(dve.tensor_reduce(wsum[:, :, 0], wgt[:, :, :], AX.X, ALU.add))
                seq.then(dve.reciprocal(wsum[:, :, :], wsum[:, :, :]))
                dve.tensor_tensor(wgt[:, :, :], wgt[:, :, :], wsum[:, :, :].to_broadcast([P, TILES, E]),
                                  ALU.mult).then_inc(wgt_ready, 1)
                yield
                dve.wait_ge(keys_made, 2 * b + 2)
                for k in range(C // 8):
                    best = cand[:, b * C + 8 * k:b * C + 8 * k + 8]
                    seq.then(dve.max(best, key[:, :]))
                    if k < C // 8 - 1:
                        seq.then(dve.match_replace(key[:, :], best, key[:, :], -1.0))
                    yield

            dve.wait_ge(ident_steps, 1)
            x_stats(0)
            for n in range(1, TILES + 1):
                if n < TILES:
                    x_stats(n)
                x_norm(n - 1)
                if n == 1:
                    dve.wait_ge(setup, 1)
                    dve.tensor_scalar(dec[:, 2, :], dec[:, 1, :], 1e-7, None, ALU.max).then_inc(setup, 1)
                if n >= 2:
                    x_low(n - 2)
            x_low(TILES - 1)
            dve.wait_ge(setup, 3 + KC)
            invert(0)
            for s in range(STEPS):
                if s + 1 < STEPS:
                    invert(s + 1)
                step(s)
            partition_mean()
            x_stats(TILES)
            x_norm(TILES)
            partition_variance(0)
            x_low(TILES)
            sequence_variance(0)
            dve.wait_ge(vectors_in, 16 * 3)
            apply_sequence_norm()
            for i in range(TILES):
                if i + 1 < TILES:
                    x_stats(TILES + 1 + i)
                    x_norm(TILES + 1 + i)
                residual(i)
                if i + 1 < TILES:
                    x_low(TILES + 1 + i)
                second_norm(i)
                if i >= 2:
                    take_logits(i - 2)
            take_logits(TILES - 2)
            take_logits(TILES - 1)
            routing = route(0)
            for s in range(STEPS, 2 * STEPS):
                step(s)
                for _ in range(1 if s < STEPS + 3 else 2):
                    next(routing, None)
            for _ in routing:
                pass
            partition_mean()
            partition_variance(1)
            sequence_variance(1)
            apply_sequence_norm()
            for n in range(TILES, 2 * TILES):
                residual(n)
                second_norm(n)
                if n >= TILES + 2:
                    take_logits(n - 2)
            take_logits(2 * TILES - 2)
            take_logits(2 * TILES - 1)
            for _ in route(1):
                pass

            seq.then(dve.tensor_scalar(cand[:, C:], cand[:, C:], -float(T), None, ALU.add))
            for k in range(C // 8):
                seq.then(dve.max(slots[:, 8 * k:8 * k + 8], cand[:, :]))
                if k < C // 8 - 1:
                    seq.then(dve.match_replace(cand[:, :], slots[:, 8 * k:8 * k + 8], cand[:, :], -1.0))
            seq.then(dve.tensor_scalar(bump[:, :], slots[:, :], MEMBER, MEMBER, ALU.is_ge, ALU.mult))
            seq.then(dve.tensor_tensor(slots[:, :], slots[:, :], bump[:, :], ALU.subtract))
            for h in range(2):
                dve.tensor_scalar(tok2[:, h, :], slots[:, :], -1.0, float(TOKENS), ALU.mult, ALU.add).then_inc(tok_ready, 1)
            dve.wait_ge(tok_turned, 1)
            dve.tensor_copy(idx[:, :], ps_g[0][:, 0:E]).then_inc(idx_ready, 1)
            dve.tensor_copy(pair_idx[0:C, :], chunk(ps_g[0][0:C, 0:E], 0, 2)).then_inc(idx_ready, 1)
            dve.tensor_copy(pair_idx[C:P, :], chunk(ps_g[0][C:P, 0:E], 1, 2)).then_inc(idx_ready, 1)

            def group(j):
                def gated(n, u):
                    dve.wait_ge(sg_ready[n], j + 1)
                    dve.wait_ge(u_ready[n], j + 1)
                    need(dve, gu_turned[n], j)
                    dve.tensor_tensor(gu[n][:, :], sg[n][:, :], ps_u[u][:, 0:I], ALU.mult).then_inc(gu_ready[n], 1)

                def turn_copy(n, src):
                    dve.wait_ge(gu_turned[n], j + 1)
                    need(dve, d_ready[n], j)
                    dve.tensor_copy(guT[n][:, :, :], src[:, 0:I].rearrange("p (c t) -> p c t", c=IC)).then_inc(guT_ready[n], 1)

                def y_odd(u):
                    dve.wait_ge(d_ready[u], j + 1)
                    dve.wait_ge(wcol_ready[u], j + 1)
                    need(dve, added, (j - 1) * ADDS + (2 * u + 2) * ADD)
                    dve.tensor_scalar(yB[u][:, :], ps_d[u][C:P, :], wcol[u][C:P, :], None, ALU.mult).then_inc(yB_ready[u], 1)

                for u in range(2):
                    dve.wait_ge(xg_full[u], 16 * (j + 1))
                    need(dve, yA_ready[u], j)
                    need(dve, yB_ready[u], j)
                    dve.tensor_copy(wcol[u][0:C, :], xg[u][0:C, bass.ds(j * 4 + (D + 2 * u), 1)])
                    dve.tensor_copy(wcol[u][C:P, :], xg[u][C:P, bass.ds(j * 4 + (D + 2 * u + 1), 1)]).then_inc(wcol_ready[u], 1)
                    gated(u, u)
                turn_copy(0, ps_ht)
                gated(2, 0)
                turn_copy(1, ps_ht)
                y_odd(0)
                turn_copy(2, ps_xt)
                y_odd(1)

            groups(dve, group)

        @block.tensor
        def _(pe):
            def turn_x(n):
                pe.wait_ge(xn_ready, n + 1)
                need(pe, xlo_ready, n - 1 if n < TILES else n)
                bank_n = n % 2 if n < TILES else 1
                for c in range(KC):
                    ins = pe.transpose(ps_t[bank_n][:, c * P:(c + 1) * P], chunk(xn[n % 2][:, :], c), ident[:, :])
                ins.then_inc(xn_turned, 1)

            def step(s):
                c, h = s % STEPS // 2, s % 2
                t = slice(h * HALF, (h + 1) * HALF)
                if s == STEPS:
                    pe.wait_ge(x2_done, TILES)
                    pe.wait_ge(logit_copied, TILES)
                if s % STEPS < 2:
                    pe.wait_ge(xlo_ready, s // STEPS * TILES + (h + 1) * TILES // 2)
                for i, (ps, free, ready) in enumerate(((ps_r, sig_done, r_ready), (ps_v, vcopy_done, v_ready),
                                                       (ps_k, kv_done, k_ready))):
                    if s == 0:
                        pe.wait_ge(lo_ready, i + 1)
                    need(pe, free, s - 1)
                    parts = []
                    for k in range(KC):
                        hi, lo = chunk(w_hi[i][:, k, :], c), chunk(w_lo[i][:, k, :], c)
                        parts += [(hi, x_hi[:, k, t]), (hi, x_lo[k][:, t]), (lo, x_hi[:, k, t])]
                    for n, (w, xp) in enumerate(parts):
                        ins = pe.matmul(ps[h][:, :], w, xp, start=(n == 0), stop=(n == len(parts) - 1))
                    ins.then_inc(ready, 1)

            def average(b, n):
                pe.wait_ge(gpart_ready, 2 * b + n + 1)
                if n == 0:
                    pe.wait_ge(sig_done, (b + 1) * STEPS)
                pe.matmul(ps_r[0][:, n:n + 1], mean_mat[:, :], gmv[:, 0:1] if n == 0 else gtmp[:, 2:3],
                          start=True, stop=True).then_inc(gmean_ready, 1)

            def project(n):
                i, b = n % TILES, n // TILES
                if i % (TILES // 2) == 0:
                    pe.wait_ge(gn_applied, b * 2 * KC + (2 * i // TILES + 1) * KC)
                if i < 2:
                    pe.wait_ge(sig_done, (b + 1) * STEPS)
                else:
                    pe.wait_ge(x2_done, n - 1)
                for c in range(KC):
                    ins = pe.matmul(ps_y[n % 2][:, :], outT[:, c, i * P:(i + 1) * P], wo_sb[:, c, :],
                                    start=(c == 0), stop=(c == KC - 1))
                ins.then_inc(y_ready, 1)

            def turn_xw(n):
                b = n // TILES
                bank_n = n % 2 if b else 0
                pe.wait_ge(xw_ready, n + 1)
                if n == 0:
                    pe.wait_ge(xlo_ready, TILES - 1)
                elif b and n < TILES + 2:
                    pe.wait_ge(keys_made, 2)
                else:
                    pe.wait_ge(xwT_ready, n - 1 if b else n)
                for c in range(KC):
                    ins = pe.transpose(ps_t[bank_n][:, c * P:(c + 1) * P], chunk(xw[n % 2][:, :], c), ident[:, :])
                ins.then_inc(xw_turned, 1)

            def router(n):
                pe.wait_ge(xwT_ready, n + 1)
                if n % TILES < 2:
                    pe.wait_ge(kv_done, (n // TILES + 1) * STEPS)
                else:
                    pe.wait_ge(logit_copied, n - 1)
                for c in range(KC):
                    ins = pe.matmul(ps_l[n % 2][:, 0:E], xwT[n % 2][:, c, :], router_sb[:, c, :],
                                    start=(c == 0), stop=(c == KC - 1))
                ins.then_inc(logit_ready, 1)

            def turn_masks(b):
                pe.wait_ge(xlo_ready, 2 * TILES)
                pe.wait_ge(xwT_ready, (b + 1) * TILES)
                pe.wait_ge(mask_ready, b + 1)
                for h in range(2):
                    for i in range(TILES // 2):
                        ins = pe.transpose(ps_t[h][0:E, i * P:(i + 1) * P], mask[:, h * (TILES // 2) + i, :], ident[:, :])
                    ins.then_inc(mask_turned, 1)

            pe.wait_ge(ident_steps, 2)
            for n in range(TILES):
                turn_x(n)
            for s in range(STEPS):
                step(s)
            turn_x(TILES)
            pe.wait_ge(const_ready, 2)
            average(0, 0)
            average(0, 1)
            pe.wait_ge(params_in, 16 * 2)
            for i in range(TILES + 2):
                if i < TILES:
                    project(i)
                if i + 1 < TILES:
                    turn_x(TILES + 1 + i)
                if 1 <= i <= TILES:
                    turn_xw(i - 1)
                if i >= 2:
                    router(i - 2)
            for s in range(STEPS, 2 * STEPS):
                step(s)
                if s == STEPS + 1:
                    turn_masks(0)
            average(1, 0)
            average(1, 1)
            for i in range(TILES + 2):
                if i < TILES:
                    project(TILES + i)
                if 1 <= i <= TILES:
                    turn_xw(TILES + i - 1)
                if i >= 2:
                    router(TILES + i - 2)
            turn_masks(1)
            pe.wait_ge(tok_ready, 2)
            pe.transpose(ps_g[0][:, 0:E], tok2[:, :, :].rearrange("e a s -> e (a s)"), ident[0:E, 0:E]).then_inc(tok_turned, 1)
            pe.wait_ge(idx_ready, 3)
            pe.wait_ge(sh_full, 16 * 3)

            def group(j):
                def weights_in(j, u, k):
                    for n in range(2 * PIECES):
                        pe.wait_ge(w_full[n], j * 96 + 16 * (u * 3 + k + 1))

                def turn_tokens(u):
                    pe.wait_ge(xg_full[u], 16 * (j + 1))
                    if u == 0:
                        need(pe, guT_ready[2], j)
                    else:
                        pe.wait_ge(xT_ready[0], j + 1)
                    for c in range(KC):
                        ins = pe.transpose(ps_xt[:, c * P:(c + 1) * P], chunk(xg[u][:, 0:D], c), ident[:, :])
                    ins.then_inc(xg_turned[u], 1)

                def gate_and_up(u):
                    pe.wait_ge(xT_ready[u], j + 1)
                    for w, (ps, ready) in enumerate(((ps_g[u], g_ready[u]), (ps_u[u], u_ready[u]))):
                        weights_in(j, u, w)
                        need(pe, (sg_ready, gu_ready)[w][1 if u else 2], j)
                        for c in range(KC):
                            for e in range(2):
                                ins = pe.matmul(ps[e * C:(e + 1) * C, 0:I], xT[u][:, c, e * C:(e + 1) * C],
                                                gate_up(u, e, w)[:, c, :], start=(c == 0), stop=(c == KC - 1))
                        ins.then_inc(ready, 1)

                def shared_gate_and_up():
                    pe.wait_ge(xS_full, 16 * (j + 1))
                    for w, (ps, ready) in enumerate(((ps_g[0], g_ready[2]), (ps_u[0], u_ready[2]))):
                        pe.wait_ge((sg_ready, gu_ready)[w][0], j + 1)
                        for c in range(KC):
                            ins = pe.matmul(ps[:, 0:I], xS[:, c, :], sh_gu[w][:, c, :],
                                            start=(c == 0), stop=(c == KC - 1))
                        ins.then_inc(ready, 1)

                def turn_gated(n, dst):
                    pe.wait_ge(gu_ready[n], j + 1)
                    if n == 0:
                        need(pe, guT_ready[1], j)
                    elif n == 1:
                        pe.wait_ge(guT_ready[0], j + 1)
                    for c in range(IC):
                        ins = pe.transpose(dst[:, c * P:(c + 1) * P], chunk(gu[n][:, :], c, IC), ident[:, :])
                    ins.then_inc(gu_turned[n], 1)

                def down_pair(u):
                    pe.wait_ge(guT_ready[u], j + 1)
                    weights_in(j, u, 2)
                    if u == 0:
                        need(pe, yS_ready, j)
                    else:
                        need(pe, yA_ready[1], j)
                        need(pe, yB_ready[1], j)
                    for c in range(IC):
                        for e in range(2):
                            ins = pe.matmul(ps_d[u][e * C:(e + 1) * C, :], guT[u][:, c, e * C:(e + 1) * C],
                                            down(u, e)[:, c, :], start=(c == 0), stop=(c == IC - 1))
                    ins.then_inc(d_ready[u], 1)

                def down_shared():
                    pe.wait_ge(guT_ready[2], j + 1)
                    pe.wait_ge(yA_ready[0], j + 1)
                    pe.wait_ge(yB_ready[0], j + 1)
                    for c in range(IC):
                        ins = pe.matmul(ps_d[0][:, :], guT[2][:, c, :], sh_dn[:, c, :],
                                        start=(c == 0), stop=(c == IC - 1))
                    ins.then_inc(d_ready[2], 1)

                turn_tokens(0)
                gate_and_up(0)
                turn_tokens(1)
                gate_and_up(1)
                turn_gated(0, ps_ht)
                shared_gate_and_up()
                down_pair(0)
                turn_gated(1, ps_ht)
                turn_gated(2, ps_xt)
                down_pair(1)
                down_shared()

            groups(pe, group)


_ARGS = ["L0_attn_x", "L0_attn_Wr", "L0_attn_Wk", "L0_attn_Wv", "L0_attn_Wo", "L0_attn_decay", "L0_attn_gn_weight",
         "L0_attn_gn_bias", "L0_ffn_w_router", "L0_ffn_w_gate", "L0_ffn_w_up", "L0_ffn_w_down",
         "L0_ffn_w_sh_gate", "L0_ffn_w_sh_up", "L0_ffn_w_sh_down"]
_SWAPPED = {"L0_attn_Wr", "L0_attn_Wk", "L0_attn_Wv", "L0_attn_Wo", "L0_ffn_w_router"}


def kernel(**inputs):
    import numpy as _np
    import concourse.bacc as _bacc
    from concourse import mybir as _mybir
    from concourse.bass_utils import run_bass_kernel_spmd as _run

    nc = _bacc.Bacc("TRN2", target_bir_lowering=False, num_devices=1)
    arrays, args = {}, []
    for name in _ARGS:
        a = _np.asarray(inputs[name])
        if name in _SWAPPED:
            a = a.T
        if name == "L0_attn_x":
            a = a.reshape(-1, a.shape[-1])
        a = _np.ascontiguousarray(a)
        arrays[f"in_{name}"] = a
        args.append(nc.dram_tensor(f"in_{name}", a.shape, _mybir.dt.from_np(a.dtype), kind="ExternalInput").ap())
    shape = inputs["L0_attn_x"].shape
    out = nc.dram_tensor("out_dram", (shape[0] * shape[1], shape[2]), F32, kind="ExternalOutput").ap()
    moe_block(nc, *args, out)
    r = _run(nc, [arrays], core_ids=[0])
    return r.results[0]["out_dram"].reshape(shape)
```

```python
from contextlib import ExitStack

import concourse.bass as bass
from concourse import mybir

F32 = mybir.dt.float32
F32R = mybir.dt.float32r
U32 = mybir.dt.uint32
I32 = mybir.dt.int32
ALU = mybir.AluOpType
ACT = mybir.ActivationFunctionType
AX = mybir.AxisListType

P = 128
SEQS, T, D = 2, 1024, 512
TOKENS = SEQS * T
KC = D // P
TILES = T // P
HALF = 512
STEPS = KC * T // HALF
E, TOPK, I, C = 64, 4, 384, 64
IC = I // P
ROW = D + E
LN_EPS = 1e-5
SENTINEL, TAKEN = -3.0e38, -3.3e38
NORMS = 2 * TILES + 1
MEMBER = 4096.0
GROUPS = E // 4
W = KC * I
PIECES = 2
ADD = 16
ADDS = 5 * ADD


def moe_block(nc, x, wr, wk, wv, wo, decay, gn_w, gn_b, w_router, w_gate, w_up, w_down,
              sh_gate, sh_up, sh_down, out):
    xw_dram = nc.dram_tensor("xw_dram", [TOKENS, ROW], F32, kind="Internal").ap()
    xt_dram = nc.dram_tensor("xt_dram", [TOKENS // P, P, D], F32, kind="Internal").ap()

    with ExitStack() as ctx:
        def sem(name):
            return ctx.enter_context(nc.semaphore(name))

        def sem2(name):
            return [sem(f"{name}{u}") for u in range(2)]

        bank = [ctx.enter_context(nc.psum_tensor(f"bank{i}", [P, 512], F32)) for i in range(8)]
        ps_r, ps_k, ps_v, ps_t = bank[0:2], bank[2:4], bank[4:6], bank[6:8]
        ps_y, ps_l, ps_mean = [ps_r[0], ps_v[0], ps_r[1], ps_v[1]], ps_k, ps_k[1]
        ps_g, ps_u, ps_xt, ps_ht, ps_d = bank[0:2], bank[2:4], bank[4], bank[5], bank[6:8]

        start = (nc.sbuf_base + 63) // 64 * 64
        top = [start]

        def room(size):
            at = top[0]
            top[0] += size
            return at

        def tile(name, shape, dt=F32, at=None):
            size = 4
            for n in shape[1:]:
                size *= n
            return nc.alloc_sbuf_tensor_at(name, shape, dt, offset=room((size + 31) // 32 * 32) if at is None else at)

        K4 = 4 * T
        ident = tile("ident", [P, P])
        mean_mat = tile("mean_mat", [P, P])
        ones = tile("ones", [P, 1])
        minus_half = tile("minus_half", [P, 1])
        dec = tile("dec", [P, 5, KC])
        gnw_sb, gnb_sb = tile("gnw_sb", [P, KC]), tile("gnb_sb", [P, KC])
        ramp = tile("ramp", [P, HALF])
        router_sb = tile("router_sb", [P, KC, E])
        wo_hi, wo_lo = tile("wo_hi", [P, KC, D], F32R), tile("wo_lo", [P, KC, D], F32R)
        row_w, row_b = tile("row_w", [P, D]), tile("row_b", [P, D])
        w_at = [room(2 * 3 * W * 4) for _ in range(2)]
        w_hi, w_lo = ([tile(f"{n}_{part}", [P, KC, D], F32R, at=w_at[0] + (3 * side + i) * 2 * K4)
                       for i, n in enumerate(("wr", "wv", "wk"))] for side, part in enumerate(("hi", "lo")))
        x_lo = [tile(f"x_lo{k}", [P, T], F32R, at=w_at[0] + 12 * K4 + k * K4) for k in range(KC)]
        ring_at = w_at[0] + 16 * K4
        RING = 4
        ring = [tile(f"ring{i}", [P, D], at=ring_at + i * 2048) for i in range(RING)]
        assert ring_at + RING * 2048 <= top[0]
        xhi_at = room(4 * K4)
        x_hi = tile("x_hi", [P, KC, T], F32R, at=xhi_at)
        scale_at, inv_at, out_at = room(4 * K4), room(4 * K4), room(8 * K4)
        scale, inv = tile("scale", [P, KC, T], at=scale_at), tile("inv", [P, KC, T], at=inv_at)
        out_hi, out_lo = (tile(f"out_{n}", [P, KC, T], F32R, at=out_at + i * 4 * K4) for i, n in enumerate(("hi", "lo")))
        raw = [tile(f"{n}_raw", [P, KC, D], at=out_at + i * 2 * K4) for i, n in enumerate(("wr", "wv", "wk", "wo"))]
        rx_at, vx_at, st_at = room(K4), room(K4), room(K4)
        r_sb = [tile(f"r_sb{u}", [P, HALF], at=rx_at + u * 2048) for u in range(2)]
        v_sb = [tile(f"v_sb{u}", [P, HALF], at=vx_at + u * 2048) for u in range(2)]
        state = [tile(f"state{u}", [P, HALF], at=st_at + u * 2048) for u in range(2)]
        carry = tile("carry", [P, KC])
        row = tile("row", [P, D], at=st_at)
        pos_i = tile("pos_i", [P, T], I32, at=st_at)
        xin_at, xn_at, xw_at = room(K4), room(K4), room(K4)
        xin = [tile(f"xin{u}", [P, D], at=xin_at + u * 2048) for u in range(2)]
        xn = [tile(f"xn{u}", [P, D], at=xn_at + u * 2048) for u in range(2)]
        kv = tile("kv", [P, HALF], at=xw_at)
        x2_second = tile("x2_second", [P, TILES, D], at=inv_at)
        x2 = [ring[n % RING] for n in range(TILES)] + [x2_second[:, n, :] for n in range(TILES)]
        xw_spots = [xw_at, xw_at + 2048, vx_at, vx_at + 2048]
        xw_ring = [tile(f"xw_ring{i}", [P, D], at=a) for i, a in enumerate(xw_spots)]
        xw = [xw_ring[n % 4] for n in range(TILES)] + [tile(f"xw{n}", [P, D], at=(xin_at if n < 2 else scale_at) + n * 2048) for n in range(TILES)]
        xwT_ring = [tile(f"xwT{i}", [P, KC, P], at=a) for i, a in enumerate((rx_at, rx_at + 2048, vx_at, vx_at + 2048))]
        xwT = [xwT_ring[n % 2] for n in range(TILES)] + [xwT_ring[n % 4] for n in range(TILES)]
        stats = tile("stats", [P, 6])
        mv = [tile(f"mv{u}", [P, 2]) for u in range(4)]
        var_eps = [tile(f"var_eps{u}", [P, 1]) for u in range(4)]
        rstd = [tile(f"rstd{u}", [P, 1]) for u in range(4)]
        neg_mean = [tile(f"neg_mean{u}", [P, 1]) for u in range(4)]
        shift = [tile(f"shift{u}", [P, 1]) for u in range(4)]
        gstats = tile("gstats", [P, STEPS, 6])
        gmv = tile("gmv", [P, 2])
        gtmp = tile("gtmp", [P, 4])
        grstd, grow = tile("grstd", [P, 1]), tile("grow", [P, 1])
        logits = tile("logits", [P, TILES, E + 4])
        top8 = tile("top8", [P, TILES, 8])
        pick8 = tile("pick8", [P, TILES, 8])
        mask = tile("mask", [P, TILES, E], at=xn_at)
        wgt = tile("wgt", [P, TILES, E], at=xn_at + 2048)
        wsum = tile("wsum", [P, TILES, 1])
        key = tile("key", [P, HALF + C])
        best = tile("best", [P, C])
        cand = tile("cand", [E, 2 * C], at=xin_at + 1024)
        slots = tile("slots", [E, C], at=xin_at + 512)
        bump = tile("bump", [E, C], at=xin_at + 768)
        tok2 = tile("tok2", [E, 2, C], at=xin_at)
        idx = tile("idx", [P, E], U32)
        pair_idx = tile("pair_idx", [P, E // 2], U32)
        gidx = [tile(f"gidx{u}", [P, 1], U32) for u in range(2)]
        sidx = [tile(f"sidx{u}", [C, 1], U32) for u in range(2)]
        wcol = [tile(f"wcol{u}", [P, 1]) for u in range(2)]
        arena_end = top[0]

        top[0] = xhi_at
        sh_sb = tile("sh_sb", [P, 3, W])
        xT = [tile(f"xT{u}", [P, KC, P]) for u in range(2)]
        xS = tile("xS", [P, KC, P], at=st_at + 2048)
        sg = [tile(f"sg{n}", [P, I]) for n in range(3)]
        gu = [tile(f"gu{n}", [P, I]) for n in range(3)]
        guT = [tile(f"guT{n}", [P, IC, P]) for n in range(3)]
        yA = [tile(f"yA{u}", [C, D]) for u in range(2)]
        yB = [tile(f"yB{u}", [C, D]) for u in range(2)]
        yS = tile("yS", [P, D])
        assert top[0] <= out_at
        w_at.append(out_at)
        assert out_at + 2 * 3 * W * 4 <= vx_at
        w_sb = [tile(f"w_sb{n}", [P, 2, 3, W], at=a) for n, a in enumerate(w_at)]
        xg = [tile(f"xg{u}", [P, ROW], at=xn_at + u * ROW * 4) for u in range(2)]
        assert xn_at + 2 * ROW * 4 <= xw_at + K4
        ctx.enter_context(nc.sbuf_tensor("arena", [P, (arena_end - nc.sbuf_base + 3) // 4], F32))

        def slot(r, u):
            return w_sb[(2 * r + u) % 3]

        def gate_up(r, u, e, which):
            return slot(r, u)[:, e, which, :].rearrange("p (c n) -> p c n", c=KC)

        def down(r, u, e):
            return slot(r, u)[:, e, 2, :].rearrange("p (c n) -> p c n", c=IC)

        sh_gu = [sh_sb[:, w, :].rearrange("p (c n) -> p c n", c=KC) for w in range(2)]
        sh_dn = sh_sb[:, 2, :].rearrange("p (c n) -> p c n", c=IC)

        def chunk(ap, c, n=KC):
            return ap.rearrange("p (m c) -> p c m", c=n)[:, c, :]

        def need(eng, s, v):
            if not isinstance(v, int) or v > 0:
                eng.wait_ge(s, v)

        dec_in, vectors_in = sem("dec_in"), sem("vectors_in")
        raw_in = [sem(f"raw_in{i}") for i in range(4)]
        router_in = sem("router_in")
        sh_full = sem("sh_full")
        ident_steps = sem("ident_steps")
        const_ready = sem("const_ready")
        setup = sem("setup")
        power_ready, inv_made = sem("power_ready"), sem("inv_made")
        hi_ready, lo_ready = sem("hi_ready"), sem("lo_ready")
        v_lo_ready = sem("v_lo_ready")
        wo_hi_ready, wo_lo_ready = sem("wo_hi_ready"), sem("wo_lo_ready")
        rows_ready, rows_copied = sem("rows_ready"), sem("rows_copied")
        xin_full, ring_full = sem2("xin_full"), [sem(f"ring_full{i}") for i in range(RING)]
        var_ready, rstd_ready = sem("var_ready"), sem("rstd_ready")
        shift_ready = sem("shift_ready")
        xn_ready = sem("xn_ready")
        xn_turned = sem("xn_turned")
        xhi_ready, xlo_ready = sem("xhi_ready"), sem("xlo_ready")
        inv_ready = sem("inv_ready")
        r_ready, k_ready, v_ready = sem("r_ready"), sem("k_ready"), sem("v_ready")
        sig_done, vcopy_done = sem("sig_done"), sem("vcopy_done")
        rscaled, vscaled = sem("rscaled"), sem("vscaled")
        kv_done, out_done = sem("kv_done"), sem("out_done")
        dve_seq = sem("dve_seq")
        pool_seq = sem("pool_seq")
        gpart_ready = sem("gpart_ready")
        gmean_ready = sem("gmean_ready")
        stat_done = sem("stat_done")
        outhi_done, outlo_done = sem("outhi_done"), sem("outlo_done")
        row_ready = sem("row_ready")
        xrow_done = sem("xrow_done")
        y_ready = sem("y_ready")
        x2_done, xw_ready = sem("x2_done"), sem("xw_ready")
        xw_turned, xwT_ready = sem("xw_turned"), sem("xwT_ready")
        logit_ready, logit_copied = sem("logit_ready"), sem("logit_copied")
        x2_stored, xw_stored, xwT_stored = ([sem(f"{n}{i}") for i in range(4)] for n in ("x2_stored", "xw_stored", "xwT_stored"))
        mask_ready, diff_ready, wgt_ready = sem("mask_ready"), sem("diff_ready"), sem("wgt_ready")
        exp_done = sem("exp_done")
        wgt_stored = sem("wgt_stored")
        masked, sums_ready = sem("masked"), sem("sums_ready")
        mask_turned, keys_made = sem("mask_turned"), sem("keys_made")
        best_ready, best_moved = sem("best_ready"), sem("best_moved")
        tok_ready, tok_turned, idx_ready = sem("tok_ready"), sem("tok_turned"), sem("idx_ready")
        w_full = [sem(f"w_full{n}") for n in range(2 * PIECES)]
        xg_full, xg_turned, xT_ready, wcol_ready = sem2("xg_full"), sem2("xg_turned"), sem2("xT_ready"), sem2("wcol_ready")
        xS_full = sem("xS_full")
        g_ready, u_ready, sg_ready, gu_ready, gu_turned, guT_ready, d_ready = (
            [sem(f"{n}{u}") for u in range(3)]
            for n in ("g_ready", "u_ready", "sg_ready", "gu_ready", "gu_turned", "guT_ready", "d_ready"))
        yA_ready, yB_ready, yS_ready = sem2("yA_ready"), sem2("yB_ready"), sem("yS_ready")
        added = sem("added")

        def xin_place(n):
            if n < TILES and n not in (4, 5):
                i = n % 6
                return ring[i], ring_full[i], 16 * (n // 6 + 1)
            return xin[n % 2], xin_full[n % 2], 16 * ((n - 4) // 2 + 1 - (n >= TILES))

        def xc_place(n):
            i = n % RING if n < TILES else (n - TILES) // 2
            before = 2 if i < 2 else 1
            return x2[n], ring_full[i], 16 * (before + (n // RING if n < TILES else TILES // RING) + 1)

        def turned_after(s):
            return {0: (4,), 1: (5, 6), 2: (7,)}.get(s, ())

        class Steps:

            def __init__(self, eng, s):
                self.eng, self.s, self.base, self.n = eng, s, 0, 0

            def then(self, ins, apart=False):
                self.n += 1
                ins.then_inc(self.s, 1)
                self.eng.wait_ge(self.s, self.base + self.n)
                if apart:
                    self.eng.nop(nofuse=True)

            def loop(self, i, per, before):
                self.base, self.n = i * per + before, 0

        block = ctx.enter_context(nc.Block())

        @block.sync
        def _(sp):
            def load_x(n, place):
                dst, full, _ = place(n)
                sp.dma_start(dst[:, :], x[n * P:(n + 1) * P, :]).then_inc(full, 16)

            def wait(s, v):
                need(sp, s, v)
                if not isinstance(v, int):
                    sp.nop(nofuse=True)

            def load_matrix(j, r, u, k):
                wait((g_ready, u_ready, d_ready)[k][1 - u], j - 1 + u)
                m = j * 6 + (u * 3 + k)
                for n in range(2 * PIECES):
                    e, h = n // PIECES, n % PIECES
                    if n < 2 * PIECES - 1:
                        wait(w_full[n + 1], m * 16)
                    else:
                        wait(w_full[0], m * 16 + 16)
                    cols = slice(h * W // PIECES, (h + 1) * W // PIECES)
                    src = (w_gate, w_up, w_down)[k][bass.ds(j * 4 + (u * 2 + e), 1)].rearrange("a (p c) n -> (a p) (c n)", p=P)
                    sp.dma_start(slot(r, u)[:, e, k, cols], src[:, cols]).then_inc(w_full[n], 16)

            def load_shared_tile(j):
                wait(u_ready[2], j)
                sp.dma_start(xS[:, :, :].rearrange("p c t -> p (c t)"),
                             xt_dram[bass.ds(j, 1)].rearrange("a p n -> (a p) n")).then_inc(xS_full, 16)

            for n in range(2):
                load_x(n, xin_place)
            sp.dma_start(dec[:, 0, :], decay.rearrange("(p c) -> p c", c=KC)).then_inc(dec_in, 16)
            for n in range(2, 4):
                load_x(n, xin_place)
            for i, w in enumerate((wr, wv, wk)):
                sp.dma_start(raw[i][:, :, :], w.rearrange("(p c) n -> p c n", c=KC)).then_inc(raw_in[i], 16)
            sp.dma_start(gnw_sb[:, :], gn_w.rearrange("(p c) -> p c", c=KC)).then_inc(vectors_in, 16)
            sp.dma_start(gnb_sb[:, :], gn_b.rearrange("(p c) -> p c", c=KC)).then_inc(vectors_in, 16)
            sp.dma_start(raw[3][:, :, :], wo.rearrange("(p c) n -> p c n", c=KC)).then_inc(raw_in[3], 16)
            for n in range(4, 6):
                load_x(n, xin_place)
            sp.dma_start(router_sb[:, :, :], w_router.rearrange("(p c) n -> p c n", c=KC)).then_inc(router_in, 16)
            for n in range(6, TILES + 2):
                sp.wait_ge(xn_ready, n - 6 + 1 if n < TILES else n - TILES + 5)
                load_x(n, xin_place)
            sp.wait_ge(xn_ready, TILES)
            for n in range(RING):
                load_x(n, xc_place)
            for n in range(RING, TILES):
                sp.wait_ge(xn_ready, TILES + n - RING + 1)
                load_x(TILES + n - 2, xin_place)
                sp.wait_ge(x2_stored[n % RING], 16)
                sp.wait_ge(xw_ready, n - RING + 1)
                load_x(n, xc_place)
            for n in range(2 * TILES - 2, 2 * TILES):
                sp.wait_ge(xn_ready, n - 1)
                load_x(n, xin_place)
            sp.wait_ge(vscaled, 2 * STEPS)
            for n in range(TILES, 2 * TILES, 2):
                sp.dma_start(x2_second[:, n - TILES:n - TILES + 2, :],
                             x[n * P:(n + 2) * P, :].rearrange("(a p) m -> p a m", p=P)).then_inc(xc_place(n)[1], 16)
            sp.wait_ge(k_ready, 2 * STEPS)
            sp.wait_ge(out_done, 2 * STEPS)
            for k in range(3):
                load_matrix(0, 0, 0, k)
            for k, w in enumerate((sh_gate, sh_up, sh_down)):
                sp.dma_start(sh_sb[:, k, :], w.rearrange("(p c) n -> p (c n)", p=P)).then_inc(sh_full, 16)
            load_shared_tile(0)
            for k in range(3):
                load_matrix(0, 0, 1, k)
            sp.wait_ge(y_ready, 2 * TILES)
            sp.wait_ge(logit_ready, 2 * TILES)
            for i in range(4):
                sp.wait_ge(xwT_stored[i], 16 * SEQS * TILES // 4)

            def load_even_pair(j, r):
                for k in range(3):
                    load_matrix(j, r, 0, k)
                    if k == 0:
                        load_shared_tile(j)

            def group(j, r, last=False):
                for k in range(3):
                    load_matrix(j, r, 1, k)
                if not last:
                    load_even_pair(j + 1, (r + 1) % 3)

            load_even_pair(1, 1)
            with sp.Fori(0, (GROUPS - 4) // 3) as i:
                for n in range(3):
                    group(i * 3 + (n + 1), (n + 1) % 3)
            for j in range(GROUPS - 3, GROUPS):
                group(j, j % 3, last=j == GROUPS - 1)

        @block.gpsimd
        def _(pool):
            seq = Steps(pool, pool_seq)
            pool.iota(pos_i[:, :], pattern=[[1, T]], base=0, channel_multiplier=0).then_inc(const_ready, 1)
            pool.memset(minus_half[:, :], -0.5)
            pool.memset(ident[:, :], 0.0).then_inc(ident_steps, 1)
            pool.wait_ge(ident_steps, 1)
            pool.affine_select(out=ident[:, :], in_=ident[:, :], compare_op=ALU.not_equal, fill=1.0,
                               base=0, pattern=[[-1, P]], channel_multiplier=1).then_inc(ident_steps, 1)
            norms = [0]

            def powers(count):
                for _ in range(count):
                    n = norms[0]
                    pool.wait_ge(var_ready, n + 1)
                    pool.tensor_tensor(rstd[n % 4][:, :], var_eps[n % 4][:, :], minus_half[:, :],
                                       ALU.pow).then_inc(rstd_ready, 1)
                    norms[0] += 1

            powers(1)
            pool.memset(mean_mat[:, :], 1.0 / P)
            pool.memset(ones[:, :], 1.0).then_inc(const_ready, 1)
            powers(3)
            for i in (0, 2):
                for c in range(KC):
                    if c == 0:
                        pool.wait_ge(hi_ready, i + 1)
                    ins = pool.tensor_tensor(w_lo[i][:, c, :], raw[i][:, c, :], w_hi[i][:, c, :].bitcast(F32), ALU.subtract)
                ins.then_inc(lo_ready, 1)
            powers(2)

            def scale_step(s):
                u, b, c = s % 2, s // STEPS, s % KC
                h = s % STEPS // KC
                t = slice(h * HALF, (h + 1) * HALF)
                pool.wait_ge(vcopy_done, s + 1)
                if b == 0:
                    pool.wait_ge(inv_ready, s + 1)
                pool.tensor_tensor(v_sb[u][:, :], v_sb[u][:, :], inv[:, c, t], ALU.mult).then_inc(vscaled, 1)
                pool.wait_ge(sig_done, s + 1)
                pool.tensor_tensor(r_sb[u][:, :], r_sb[u][:, :], scale[:, c, t], ALU.mult).then_inc(rscaled, 1)

            def out_low(s):
                u, c, h = s % 2, s % KC, s % STEPS // KC
                t = slice(h * HALF, (h + 1) * HALF)
                pool.wait_ge(outhi_done, s + 1)
                pool.tensor_tensor(out_lo[:, c, t], r_sb[u][:, :], out_hi[:, c, t].bitcast(F32),
                                   ALU.subtract).then_inc(outlo_done, 1)

            def add_row(n):
                b = n // TILES
                _, full, value = xc_place(n)
                pool.wait_ge(row_ready, b + 1)
                pool.wait_ge(full, value)
                pool.tensor_tensor(x2[n][:, :], x2[n][:, :], row[:, :], ALU.add).then_inc(xrow_done, 1)

            def mask_weights(b):
                pool.wait_ge(exp_done, b + 1)
                pool.wait_ge(mask_ready, 2 * (b + 1))
                pool.tensor_tensor(wgt[:, :, :], wgt[:, :, :], mask[:, :, :], ALU.mult).then_inc(masked, 1)

            def scale_weights(b):
                pool.wait_ge(sums_ready, b + 1)
                pool.tensor_tensor(wgt[:, :, :], wgt[:, :, :], wsum[:, :, :].to_broadcast([P, TILES, E]),
                                   ALU.mult).then_inc(wgt_ready, 1)

            def shift_x():
                u = norms[0] % 4
                powers(1)
                pool.wait_ge(rstd_ready, norms[0])
                pool.tensor_tensor(shift[u][:, :], neg_mean[u][:, :], rstd[u][:, :], ALU.mult).then_inc(shift_ready, 1)

            def store_weights(b):
                pool.wait_ge(wgt_ready, b + 1)
                pool.dma_start(xw_dram[b * T:(b + 1) * T, D:ROW].rearrange("(i p) e -> p i e", p=P),
                               wgt[:, :, :]).then_inc(wgt_stored, 16)

            for s in range(STEPS):
                scale_step(s)
                if s < 2:
                    powers(1)
                if s == 1:
                    pool.memset(logits[:, :, E:], SENTINEL)
                    pool.memset(pick8[:, :, TOPK:], SENTINEL)
                    pool.iota(ramp[:, :], pattern=[[-1, HALF]], base=TOKENS, channel_multiplier=0,
                              allow_small_or_imprecise_dtypes=True).then_inc(const_ready, 1)
                if s:
                    out_low(s - 1)
            out_low(STEPS - 1)
            powers(2)
            add_row(0)
            add_row(1)
            for i in range(TILES):
                powers(1)
                if i + 1 < TILES:
                    shift_x()
                if i + 2 < TILES:
                    add_row(i + 2)
            for s in range(STEPS, 2 * STEPS):
                scale_step(s)
                if s > STEPS:
                    out_low(s - 1)
                if s == STEPS + 2:
                    mask_weights(0)
                if s == STEPS + 4:
                    scale_weights(0)
                    store_weights(0)
            out_low(2 * STEPS - 1)
            powers(1)
            add_row(TILES)
            add_row(TILES + 1)
            for n in range(TILES, 2 * TILES):
                powers(1)
                if n + 2 < 2 * TILES:
                    add_row(n + 2)
            mask_weights(1)
            scale_weights(1)
            store_weights(1)

            def gather(j, u):
                need(pool, xg_turned[u], j)
                need(pool, wcol_ready[u], j)
                seq.then(pool.tensor_copy(gidx[u][:, :], pair_idx[:, bass.ds(j * 2 + u, 1)]), apart=True)
                pool.indirect_dma_start(out=xg[u][:, :], out_offset=None, in_=xw_dram[:, :],
                                        in_offset=bass.IndirectOffsetOnAxis(ap=gidx[u][:, :], axis=0),
                                        ).then_inc(xg_full[u], 16)

            def add_group(j):
                pool.wait_ge(yS_ready, j + 1)
                need(pool, added, j * ADDS)
                if not isinstance(j, int):
                    pool.nop(nofuse=True)
                pool.dma_start(out[bass.ds(j * P, P), :], yS[:, :], accum_op=ALU.add).then_inc(added, ADD)
                n = 1
                for u in range(2):
                    for e, (y, ready) in enumerate(((yA, yA_ready), (yB, yB_ready))):
                        pool.wait_ge(ready[u], j + 1)
                        seq.then(pool.tensor_copy(sidx[e][:, :], idx[0:C, bass.ds(j * 4 + u * 2 + e, 1)]), apart=True)
                        need(pool, added, j * ADDS + n * ADD)
                        pool.nop(nofuse=True)
                        pool.indirect_dma_start(out=out[:, :],
                                                out_offset=bass.IndirectOffsetOnAxis(ap=sidx[e][:, :], axis=0),
                                                in_=y[u][:, :], in_offset=None,
                                                compute_op=ALU.add).then_inc(added, ADD)
                        n += 1
            for i in range(4):
                pool.wait_ge(x2_stored[i], 16 * SEQS * TILES // 4)
                pool.wait_ge(xw_stored[i], 16 * SEQS * TILES // 4)
            pool.wait_ge(wgt_stored, 16 * SEQS)
            pool.wait_ge(idx_ready, 3)
            for u in range(2):
                gather(0, u)
            for u in range(2):
                gather(1, u)
            add_group(0)
            before = seq.n
            with pool.Fori(1, GROUPS - 1) as j:
                seq.loop(j - 1, 6, before)
                for u in range(2):
                    gather(j + 1, u)
                add_group(j)
            seq.base, seq.n = 0, before + 6 * (GROUPS - 2)
            add_group(GROUPS - 1)
            pool.wait_ge(added, GROUPS * ADDS)

        @block.scalar
        def _(act):
            def turned_x(n):
                bank_n = n % 2 if n < TILES else 1
                act.wait_ge(xn_turned, n + 1)
                if n == TILES:
                    act.wait_ge(k_ready, STEPS)
                i = n % TILES
                act.activation(x_hi[:, :, i * P:(i + 1) * P], ps_t[bank_n][:, :].rearrange("p (c t) -> p c t", c=KC),
                               ACT.Copy).then_inc(xhi_ready, 1)

            def step(s):
                u = s % 2
                act.wait_ge(r_ready, s + 1)
                need(act, outlo_done, s - 1)
                need(act, stat_done, s - 1)
                if s == STEPS:
                    act.wait_ge(logit_ready, TILES)
                    for i in range(4):
                        act.wait_ge(xwT_stored[i], 16 * TILES // 4)
                act.activation(r_sb[u][:, :], ps_r[u][:, :], ACT.Sigmoid).then_inc(sig_done, 1)
                act.wait_ge(v_ready, s + 1)
                need(act, kv_done, s - 1)
                if s == STEPS:
                    act.wait_ge(xw_turned, TILES)
                    for i in range(4):
                        act.wait_ge(xw_stored[i], 16 * TILES // 4)
                act.activation(v_sb[u][:, :], ps_v[u][:, :], ACT.Copy).then_inc(vcopy_done, 1)

            def out_high(s):
                u, c, h = s % 2, s % KC, s % STEPS // KC
                act.wait_ge(out_done, s + 1)
                if s == 0:
                    act.wait_ge(lo_ready, 2)
                    act.wait_ge(v_lo_ready, 1)
                if s == STEPS:
                    act.wait_ge(y_ready, TILES)
                act.activation(out_hi[:, c, h * HALF:(h + 1) * HALF], r_sb[u][:, :], ACT.Copy).then_inc(outhi_done, 1)

            def norm_x(n, m):
                u = (TILES + 2 + m) % 4
                act.wait_ge(shift_ready, n - TILES)
                act.wait_ge(xn_turned, n - 1)
                act.activation(xn[n % 2][:, :], xin_place(n)[0][:, :], ACT.Identity, scale=rstd[u][:, :],
                               bias=shift[u][:, :]).then_inc(xn_ready, 1)

            def turned_xw(n):
                b = n // TILES
                rows = slice(n * P, (n + 1) * P)
                act.wait_ge(x2_done, n + 1)
                act.dma_start(out[rows, :], x2[n][:, :]).then_inc(x2_stored[n % 4], 16)
                act.wait_ge(xw_ready, n + 1)
                act.dma_start(xw_dram[rows, 0:D], xw[n][:, :]).then_inc(xw_stored[n % 4], 16)
                act.wait_ge(xw_turned, n + 1)
                if n % TILES == 0:
                    act.wait_ge(outlo_done, (b + 1) * STEPS)
                last = n - (2 if n < TILES else 4)
                if 0 <= last and not TILES <= n < TILES + 4:
                    act.wait_ge(logit_ready, last + 1)
                    act.wait_ge(xwT_stored[last % 4], 16 * (last // 4 + 1))
                act.activation(xwT[n][:, :, :], ps_t[n % 2 if b else 0][:, :].rearrange("p (c t) -> p c t", c=KC),
                               ACT.Copy).then_inc(xwT_ready, 1)
                act.wait_ge(xwT_ready, n + 1)
                act.dma_start(xt_dram[n], xwT[n][:, :, :].rearrange("p c t -> p (c t)")).then_inc(xwT_stored[n % 4], 16)

            def exponentials(b):
                act.wait_ge(diff_ready, 2 * (b + 1))
                act.activation(wgt[:, :, :], wgt[:, :, :], ACT.Exp).then_inc(exp_done, 1)

            def output_weights():
                act.wait_ge(rows_ready, 1)
                act.activation(row_w[:, :], ps_v[1][:, :], ACT.Copy).then_inc(rows_copied, 1)
                act.wait_ge(rows_ready, 2)
                act.activation(row_b[:, :], ps_k[1][:, :], ACT.Copy).then_inc(rows_copied, 1)
                act.wait_ge(vectors_in, 16 * 2)
                act.wait_ge(raw_in[3], 16)
                for c in range(KC):
                    act.activation(wo_hi[:, c, :], raw[3][:, c, :], ACT.Copy, scale=gnw_sb[:, c:c + 1]).then_inc(wo_hi_ready, 1)

            act.wait_ge(dec_in, 16)
            act.activation(dec[:, 1, :], dec[:, 0, :], ACT.Sigmoid).then_inc(setup, 1)
            def high(n):
                act.wait_ge(raw_in[n], 16)
                act.activation(w_hi[n][:, :, :], raw[n][:, :, :], ACT.Copy).then_inc(hi_ready, 1)

            turned_x(0)
            high(0)
            turned_x(1)
            act.wait_ge(setup, 2)
            act.activation(dec[:, 3, :], dec[:, 2, :], ACT.Ln).then_inc(setup, 1)
            high(1)
            turned_x(2)
            turned_x(3)
            high(2)
            act.wait_ge(setup, 3)
            act.wait_ge(const_ready, 1)
            for c in range(KC):
                act.activation(scale[:, c, :], pos_i[:, :], ACT.Exp, scale=dec[:, 3, c:c + 1]).then_inc(setup, 1)
            for c in range(KC):
                act.wait_ge(power_ready, c + 1)
                act.activation(inv[:, c, :], inv[:, c, :], ACT.Exp).then_inc(inv_made, 1)
            for s in range(STEPS):
                step(s)
                if s == 0:
                    output_weights()
                else:
                    out_high(s - 1)
                for n in turned_after(s):
                    turned_x(n)
            out_high(STEPS - 1)
            turned_x(TILES)
            norm_x(TILES + 1, 1)
            for i in range(TILES):
                turned_xw(i)
                if i + 1 < TILES:
                    turned_x(TILES + 1 + i)
                if i + 2 < TILES:
                    norm_x(TILES + 2 + i, 3 + 2 * i)
            for s in range(STEPS, 2 * STEPS):
                step(s)
                if s > STEPS:
                    out_high(s - 1)
                if s == STEPS + 1:
                    exponentials(0)
            out_high(2 * STEPS - 1)
            for n in range(TILES, 2 * TILES):
                turned_xw(n)
            exponentials(1)

            def turned_tokens(j, u):
                act.wait_ge(xg_turned[u], j + 1)
                need(act, u_ready[u], j)
                act.activation(xT[u][:, :, :], ps_xt[:, :].rearrange("p (c t) -> p c t", c=KC),
                               ACT.Copy).then_inc(xT_ready[u], 1)

            def silu(j, n, u):
                act.wait_ge(g_ready[n], j + 1)
                need(act, gu_ready[n], j)
                act.activation(sg[n][:, :], ps_g[u][:, 0:I], ACT.Silu).then_inc(sg_ready[n], 1)

            def group(j, last=False):
                def y_even(u):
                    act.wait_ge(d_ready[u], j + 1)
                    act.wait_ge(wcol_ready[u], j + 1)
                    need(act, added, (j - 1) * ADDS + (2 * u + 2) * ADD)
                    act.activation(yA[u][:, :], ps_d[0][0:C, :], ACT.Copy, scale=wcol[u][0:C, :]).then_inc(yA_ready[u], 1)

                if not isinstance(j, int) or j:
                    silu(j, 2, 1)
                silu(j, 0, 0)
                act.wait_ge(d_ready[2], j + 1)
                need(act, added, (j - 1) * ADDS + ADD)
                act.activation(yS[:, :], ps_d[1][:, :], ACT.Copy).then_inc(yS_ready, 1)
                y_even(0)
                if not last:
                    turned_tokens(j + 1, 0)
                silu(j, 1, 0)
                if not last:
                    turned_tokens(j + 1, 1)
                y_even(1)

            for i in range(4):
                act.wait_ge(xw_stored[i], 16 * SEQS * TILES // 4)
            silu(0, 2, 1)
            for u in range(2):
                turned_tokens(0, u)
            group(0)
            with act.Fori(1, GROUPS - 1) as j:
                group(j)
            group(GROUPS - 1, last=True)

        @block.vector
        def _(dve):
            seq = Steps(dve, dve_seq)
            norms = [0, 0]

            def give_variance(var):
                dve.tensor_scalar(var_eps[norms[0] % 4][:, :], var, LN_EPS, None, ALU.add).then_inc(var_ready, 1)
                norms[0] += 1

            def take_power():
                norms[1] += 1
                dve.wait_ge(rstd_ready, norms[1])
                return rstd[(norms[1] - 1) % 4]

            def row_stats(src, shifted=False):
                u = norms[0] % 4
                seq.then(dve.bn_stats(stats[:, :], src[:, :]))
                seq.then(dve.bn_aggr(mv[u][:, :], stats[:, :]))
                if shifted:
                    seq.then(dve.tensor_scalar(neg_mean[u][:, :], mv[u][:, 0:1], -1.0, None, ALU.mult))
                give_variance(mv[u][:, 1:2])

            def normalise(src, dst):
                u = norms[1] % 4
                r = take_power()
                return dve.tensor_scalar(dst[:, :], src[:, :], mv[u][:, 0:1], r[:, :], ALU.subtract, ALU.mult)

            def x_stats(n):
                x_tile, full, value = xin_place(n)
                dve.wait_ge(full, value)
                row_stats(x_tile, shifted=n > TILES)

            def x_norm(n):
                need(dve, xn_turned, n - 1)
                normalise(xin_place(n)[0], xn[n % 2]).then_inc(xn_ready, 1)

            def x_low(n):
                bank_n = n % 2 if n < TILES else 1
                i = n % TILES
                dve.wait_ge(xhi_ready, n + 1)
                if n == TILES:
                    dve.wait_ge(k_ready, STEPS)
                for k in range(KC):
                    t = slice(i * P, (i + 1) * P)
                    ins = dve.tensor_tensor(x_lo[k][:, t], ps_t[bank_n][:, k * P:(k + 1) * P],
                                            x_hi[:, k, t].bitcast(F32), ALU.subtract)
                ins.then_inc(xlo_ready, 1)

            def invert(s):
                c, h = s % KC, s // KC
                t = slice(h * HALF, (h + 1) * HALF)
                dve.tensor_scalar(inv[:, c, t], inv[:, c, t], 1e10, None, ALU.min).then_inc(inv_ready, 1)

            def step(s):
                u, c, h = s % 2, s % KC, s % STEPS // KC
                dve.wait_ge(k_ready, s + 1)
                dve.wait_ge(vscaled, s + 1)
                dve.tensor_tensor(kv[:, :], ps_k[u][:, :], v_sb[u][:, :], ALU.mult).then_inc(kv_done, 1)
                dve.wait_ge(kv_done, s + 1)
                seq.then(dve.tensor_tensor_scan(state[u][:, :], ones[:, :].to_broadcast([P, HALF]), kv[:, :],
                                                0.0 if h == 0 else carry[:, c:c + 1], ALU.mult, ALU.add))
                if h == 0:
                    seq.then(dve.tensor_copy(carry[:, c:c + 1], state[u][:, HALF - 1:HALF]))
                dve.wait_ge(rscaled, s + 1)
                dve.tensor_tensor(r_sb[u][:, :], state[u][:, :], r_sb[u][:, :], ALU.mult).then_inc(out_done, 1)
                dve.wait_ge(out_done, s + 1)
                dve.bn_stats(gstats[:, s % STEPS, :], r_sb[u][:, :]).then_inc(stat_done, 1)

            def partition_mean(b):
                dve.wait_ge(stat_done, (b + 1) * STEPS)
                dve.nop(nofuse=True)
                dve.bn_aggr(gmv[:, :], gstats[:, :, :].rearrange("p a b -> p (a b)")).then_inc(gpart_ready, 1)

            def partition_variance(b):
                dve.wait_ge(gmean_ready, 2 * b + 1)
                dve.wait_ge(gpart_ready, 2 * b + 1)
                seq.then(dve.tensor_copy(gtmp[:, 0:1], ps_mean[:, 0:1]))
                seq.then(dve.tensor_tensor(gtmp[:, 1:2], gmv[:, 0:1], gtmp[:, 0:1], ALU.subtract))
                dve.scalar_tensor_tensor(out=gtmp[:, 2:3], in0=gtmp[:, 1:2], scalar=gtmp[:, 1:2], in1=gmv[:, 1:2],
                                         op0=ALU.mult, op1=ALU.add).then_inc(gpart_ready, 1)

            def sequence_variance(b):
                dve.wait_ge(gmean_ready, 2 * b + 2)
                give_variance(ps_mean[:, 1:2])

            def sequence_row(b):
                seq.then(dve.tensor_copy(grstd[:, :], take_power()[:, :]))
                seq.then(dve.tensor_tensor(grow[:, :], gtmp[:, 0:1], grstd[:, :], ALU.mult))
                if b == 0:
                    dve.wait_ge(rows_copied, 2)
                seq.then(dve.tensor_scalar(row[:, :], row_w[:, :], grow[:, :], None, ALU.mult))
                dve.tensor_tensor(row[:, :], row_b[:, :], row[:, :], ALU.subtract).then_inc(row_ready, 1)

            def residual(n):
                dve.wait_ge(y_ready, n + 1)
                dve.wait_ge(xrow_done, n + 1)
                dve.scalar_tensor_tensor(out=x2[n][:, :], in0=ps_y[n % 4][:, :], scalar=grstd[:, :], in1=x2[n][:, :],
                                         op0=ALU.mult, op1=ALU.add).then_inc(x2_done, 1)
                dve.wait_ge(x2_done, n + 1)
                row_stats(x2[n])

            def second_norm(n):
                if 4 <= n < TILES:
                    dve.wait_ge(xw_turned, n - 3)
                    dve.wait_ge(xw_stored[n % 4], 16)
                normalise(x2[n], xw[n]).then_inc(xw_ready, 1)

            def take_logits(n):
                dve.wait_ge(logit_ready, n + 1)
                dve.tensor_copy(logits[:, n % TILES, 0:E], ps_l[n % 2][:, 0:E]).then_inc(logit_copied, 1)

            def pick(b, h):
                tiles = slice(h * TILES // 2, (h + 1) * TILES // 2)
                dve.wait_ge(logit_copied, b * TILES + tiles.stop)
                for i in range(tiles.start, tiles.stop):
                    dve.max(top8[:, i, :], logits[:, i, 0:E]).then_inc(dve_seq, 1)
                    seq.n += 1
                dve.wait_ge(dve_seq, seq.n)
                seq.then(dve.tensor_copy(pick8[:, tiles, 0:TOPK], top8[:, tiles, 0:TOPK]))
                dve.wait_ge(xn_turned, 2 * TILES)
                need(dve, wgt_stored, 16 * b)
                dve.tensor_tensor(wgt[:, tiles, :], logits[:, tiles, 0:E],
                                  top8[:, tiles, 0:1].to_broadcast([P, TILES // 2, E]), ALU.subtract).then_inc(diff_ready, 1)
                dve.wait_ge(diff_ready, 2 * b + h + 1)
                for i in range(tiles.start, tiles.stop):
                    dve.match_replace(logits[:, i, :], pick8[:, i, :], logits[:, i, :], TAKEN).then_inc(dve_seq, 1)
                    seq.n += 1
                dve.wait_ge(dve_seq, seq.n)
                dve.tensor_scalar(mask[:, tiles, :], logits[:, tiles, 0:E], TAKEN, None, ALU.is_equal).then_inc(mask_ready, 1)
                seq.then(dve.memset(logits[:, tiles, E:], SENTINEL))

            def make_keys(b):
                dve.wait_ge(mask_turned, 2 * (b + 1))
                dve.scalar_tensor_tensor(out=key[:, 0:HALF], in0=ps_t[0][:, :], scalar=MEMBER, in1=ramp[:, :],
                                         op0=ALU.mult, op1=ALU.add).then_inc(keys_made, 1)
                dve.wait_ge(keys_made, b + 1)

            def best_rounds(b, rounds):
                keys = key[:, 0:HALF + b * C]
                for k in rounds:
                    found = best[:, 8 * k:8 * k + 8]
                    if k < C // 8 - 1:
                        seq.then(dve.max(found, keys))
                        seq.then(dve.match_replace(keys, found, keys, -1.0))
                    else:
                        dve.max(found, keys).then_inc(best_ready, 1)
                        dve.wait_ge(best_ready, b + 1)

            def weight_sums(b):
                dve.wait_ge(masked, b + 1)
                seq.then(dve.tensor_reduce(wsum[:, :, 0], wgt[:, :, :], AX.X, ALU.add))
                dve.reciprocal(wsum[:, :, :], wsum[:, :, :]).then_inc(sums_ready, 1)

            def halves_together():
                seq.then(dve.tensor_copy(cand[:, 0:C], best[0:E, :]))
                dve.wait_ge(best_moved, 1)
                seq.then(dve.tensor_copy(cand[:, C:], ps_t[1][0:E, 0:C]))

            def merge_rounds(rounds):
                for k in rounds:
                    found = key[0:E, HALF + 8 * k:HALF + 8 * k + 8]
                    seq.then(dve.max(found, cand[:, :]))
                    if k < C // 8 - 1:
                        seq.then(dve.match_replace(cand[:, :], found, cand[:, :], -1.0))

            dve.wait_ge(ident_steps, 1)
            x_stats(0)
            for n in range(1, 4):
                x_stats(n)
                x_norm(n - 1)
                if n == 1:
                    dve.wait_ge(setup, 1)
                    dve.tensor_scalar(dec[:, 2, :], dec[:, 1, :], 1e-7, None, ALU.max).then_inc(setup, 1)
                else:
                    x_low(n - 2)
            x_norm(3)
            x_low(2)
            x_low(3)
            dve.wait_ge(hi_ready, 2)
            for c in range(KC):
                ins = dve.tensor_tensor(w_lo[1][:, c, :], raw[1][:, c, :], w_hi[1][:, c, :].bitcast(F32), ALU.subtract)
            ins.then_inc(v_lo_ready, 1)
            dve.wait_ge(setup, 3)
            seq.then(dve.tensor_scalar(dec[:, 4, :], dec[:, 3, :], -1.0, None, ALU.mult))
            for c in range(KC):
                dve.tensor_scalar(inv[:, c, :], pos_i[:, :], dec[:, 4, c:c + 1], 30.0,
                                  ALU.mult, ALU.min).then_inc(power_ready, 1)
            for n in (4, 5):
                x_stats(n)
                x_norm(n)
            dve.wait_ge(inv_made, KC)
            invert(0)
            dve.wait_ge(const_ready, 2)
            for s in range(STEPS):
                if s + 1 < STEPS:
                    invert(s + 1)
                if s in (1, 2):
                    for c in (2 * s - 2, 2 * s - 1):
                        dve.wait_ge(wo_hi_ready, c + 1)
                        dve.scalar_tensor_tensor(out=wo_lo[:, c, :], in0=raw[3][:, c, :], scalar=gnw_sb[:, c:c + 1],
                                                 in1=wo_hi[:, c, :].bitcast(F32), op0=ALU.mult,
                                                 op1=ALU.subtract).then_inc(wo_lo_ready, 1)
                step(s)
                for n in turned_after(s):
                    x_low(n)
                if s < 2:
                    x_stats(6 + s)
                    x_norm(6 + s)
            partition_mean(0)
            x_stats(TILES)
            partition_variance(0)
            x_norm(TILES)
            sequence_variance(0)
            sequence_row(0)
            x_low(TILES)
            residual(0)
            x_stats(TILES + 1)
            for i in range(TILES):
                second_norm(i)
                if i + 1 < TILES:
                    norms[1] += 1
                    residual(i + 1)
                    if i + 2 < TILES:
                        x_stats(TILES + 2 + i)
                if i >= 1:
                    take_logits(i - 1)
                if i + 1 < TILES:
                    x_low(TILES + 1 + i)
            take_logits(TILES - 1)
            dve.wait_ge(const_ready, 3)
            seq.then(dve.tensor_scalar(ramp[E:P, :], ramp[E:P, :], -float(HALF), None, ALU.add))
            for s in range(STEPS, 2 * STEPS):
                step(s)
                if s == STEPS:
                    pick(0, 0)
                    pick(0, 1)
                elif s == STEPS + 1:
                    make_keys(0)
                    best_rounds(0, range(2))
                elif s == STEPS + 2:
                    best_rounds(0, range(2, 5))
                elif s == STEPS + 3:
                    weight_sums(0)
                    best_rounds(0, range(5, 8))
                elif s == STEPS + 5:
                    halves_together()
                    merge_rounds(range(4))
                elif s == STEPS + 6:
                    merge_rounds(range(4, 8))
                    seq.then(dve.memset(key[E:P, HALF:], -1.0))
                    seq.then(dve.tensor_scalar(ramp[:, :], ramp[:, :], -float(T), None, ALU.add))
            partition_mean(1)
            partition_variance(1)
            sequence_variance(1)
            sequence_row(1)
            residual(TILES)
            for n in range(TILES, 2 * TILES):
                if n + 1 < 2 * TILES:
                    residual(n + 1)
                second_norm(n)
                if n > TILES:
                    take_logits(n - 1)
                if n == TILES + TILES // 2:
                    pick(1, 0)
            take_logits(2 * TILES - 1)
            pick(1, 1)
            make_keys(1)
            best_rounds(1, range(2))
            weight_sums(1)
            best_rounds(1, range(2, 8))
            dve.wait_ge(best_moved, 2)
            seq.then(dve.tensor_tensor(slots[:, :], best[0:E, :], ps_t[1][0:E, C - 1::-1], ALU.max))
            seq.then(dve.tensor_scalar(bump[:, :], slots[:, :], MEMBER, MEMBER, ALU.is_ge, ALU.mult))
            seq.then(dve.tensor_tensor(slots[:, :], slots[:, :], bump[:, :], ALU.subtract))
            for h in range(2):
                dve.tensor_scalar(tok2[:, h, :], slots[:, :], -1.0, float(TOKENS), ALU.mult, ALU.add).then_inc(tok_ready, 1)
            dve.wait_ge(tok_turned, 1)
            dve.tensor_copy(idx[:, :], ps_g[0][:, 0:E]).then_inc(idx_ready, 1)
            dve.tensor_copy(pair_idx[0:C, :], chunk(ps_g[0][0:C, 0:E], 0, 2)).then_inc(idx_ready, 1)
            dve.tensor_copy(pair_idx[C:P, :], chunk(ps_g[0][C:P, 0:E], 1, 2)).then_inc(idx_ready, 1)

            def gated(j, n, u):
                dve.wait_ge(sg_ready[n], j + 1)
                dve.wait_ge(u_ready[n], j + 1)
                need(dve, gu_turned[n], j)
                dve.tensor_tensor(gu[n][:, :], sg[n][:, :], ps_u[u][:, 0:I], ALU.mult).then_inc(gu_ready[n], 1)

            def group(j):
                def turn_copy(n, src):
                    dve.wait_ge(gu_turned[n], j + 1)
                    need(dve, d_ready[n], j)
                    dve.tensor_copy(guT[n][:, :, :], src[:, 0:I].rearrange("p (c t) -> p c t", c=IC)).then_inc(guT_ready[n], 1)

                def y_odd(u):
                    dve.wait_ge(d_ready[u], j + 1)
                    dve.wait_ge(wcol_ready[u], j + 1)
                    need(dve, added, (j - 1) * ADDS + (2 * u + 3) * ADD)
                    dve.tensor_scalar(yB[u][:, :], ps_d[0][C:P, :], wcol[u][C:P, :], None, ALU.mult).then_inc(yB_ready[u], 1)

                for u in range(2):
                    dve.wait_ge(xg_full[u], 16 * (j + 1))
                    need(dve, yA_ready[u], j)
                    need(dve, yB_ready[u], j)
                    dve.tensor_copy(wcol[u][0:C, :], xg[u][0:C, bass.ds(j * 4 + (D + 2 * u), 1)])
                    dve.tensor_copy(wcol[u][C:P, :], xg[u][C:P, bass.ds(j * 4 + (D + 2 * u + 1), 1)]).then_inc(wcol_ready[u], 1)
                gated(j, 2, 1)
                gated(j, 0, 0)
                turn_copy(2, ps_xt)
                turn_copy(0, ps_ht)
                y_odd(0)
                gated(j, 1, 0)
                turn_copy(1, ps_ht)
                y_odd(1)

            group(0)
            with dve.Fori(1, GROUPS) as j:
                group(j)

        @block.tensor
        def _(pe):
            def turn_x(n):
                pe.wait_ge(xn_ready, n + 1)
                need(pe, xlo_ready, n - 1 if n < TILES else n)
                bank_n = n % 2 if n < TILES else 1
                for c in range(KC):
                    ins = pe.transpose(ps_t[bank_n][:, c * P:(c + 1) * P], chunk(xn[n % 2][:, :], c), ident[:, :])
                ins.then_inc(xn_turned, 1)

            def output_rows():
                pe.wait_ge(vectors_in, 16 * 2)
                pe.wait_ge(raw_in[3], 16)
                for ps, vector in ((ps_v[1], gnw_sb), (ps_k[1], gnb_sb)):
                    for c in range(KC):
                        ins = pe.matmul(ps[:, :], vector[:, c:c + 1].to_broadcast([P, P]), raw[3][:, c, :],
                                        start=(c == 0), stop=(c == KC - 1))
                    ins.then_inc(rows_ready, 1)

            def step(s):
                u, c, h = s % 2, s % KC, s % STEPS // KC
                t = slice(h * HALF, (h + 1) * HALF)
                if s == STEPS:
                    pe.wait_ge(x2_done, TILES)
                    pe.wait_ge(logit_copied, TILES)
                if s % STEPS in (0, KC):
                    pe.wait_ge(xlo_ready, s // STEPS * TILES + (h + 1) * TILES // 2)
                for i, (ps, free, ready) in enumerate(((ps_r, sig_done, r_ready), (ps_v, vcopy_done, v_ready),
                                                       (ps_k, kv_done, k_ready))):
                    if s == 0:
                        pe.wait_ge((lo_ready, v_lo_ready, lo_ready)[i], (1, 1, 2)[i])
                    need(pe, free, s - 1)
                    if s == 1 and i:
                        pe.wait_ge(rows_copied, i)
                    parts = []
                    for k in range(KC):
                        hi, lo = chunk(w_hi[i][:, k, :], c), chunk(w_lo[i][:, k, :], c)
                        parts += [(hi, x_hi[:, k, t]), (hi, x_lo[k][:, t]), (lo, x_hi[:, k, t])]
                    for n, (w, xp) in enumerate(parts):
                        ins = pe.matmul(ps[u][:, :], w, xp, start=(n == 0), stop=(n == len(parts) - 1))
                    ins.then_inc(ready, 1)

            def average(b, n):
                pe.wait_ge(gpart_ready, 2 * b + n + 1)
                pe.matmul(ps_mean[:, n:n + 1], mean_mat[:, :], gmv[:, 0:1] if n == 0 else gtmp[:, 2:3],
                          start=True, stop=True).then_inc(gmean_ready, 1)

            def project(n):
                i, b = n % TILES, n // TILES
                if i in (0, 4):
                    pe.wait_ge(outlo_done, b * STEPS + (KC if i == 0 else STEPS))
                if i < 4:
                    pe.wait_ge((sig_done, vcopy_done)[i % 2], (b + 1) * STEPS - 1 + i // 2)
                if i >= 4:
                    pe.wait_ge(x2_done, n - 3)
                parts = []
                for c in range(KC):
                    hi, lo = out_hi[:, c, i * P:(i + 1) * P], out_lo[:, c, i * P:(i + 1) * P]
                    parts += [(hi, wo_hi[:, c, :]), (hi, wo_lo[:, c, :]), (lo, wo_hi[:, c, :])]
                for m, (o, w) in enumerate(parts):
                    ins = pe.matmul(ps_y[n % 4][:, :], o, w, start=(m == 0), stop=(m == len(parts) - 1))
                ins.then_inc(y_ready, 1)

            def turn_xw(n):
                b = n // TILES
                bank_n = n % 2 if b else 0
                pe.wait_ge(xw_ready, n + 1)
                if n == 0:
                    pe.wait_ge(xlo_ready, TILES - 1)
                elif b and n < TILES + 2:
                    pe.wait_ge(keys_made, 1)
                else:
                    pe.wait_ge(xwT_ready, n - 1 if b else n)
                for c in range(KC):
                    ins = pe.transpose(ps_t[bank_n][:, c * P:(c + 1) * P], chunk(xw[n][:, :], c), ident[:, :])
                ins.then_inc(xw_turned, 1)

            def router(n):
                pe.wait_ge(xwT_ready, n + 1)
                if n % TILES < 2:
                    pe.wait_ge(kv_done, (n // TILES + 1) * STEPS)
                else:
                    pe.wait_ge(logit_copied, n - 1)
                for c in range(KC):
                    ins = pe.matmul(ps_l[n % 2][:, 0:E], xwT[n][:, c, :], router_sb[:, c, :],
                                    start=(c == 0), stop=(c == KC - 1))
                ins.then_inc(logit_ready, 1)

            def turn_masks(b):
                pe.wait_ge(xlo_ready, 2 * TILES)
                pe.wait_ge(xwT_ready, (b + 1) * TILES)
                for h in range(2):
                    pe.wait_ge(mask_ready, 2 * b + h + 1)
                    for i in range(TILES // 2):
                        ins = pe.matmul(ps_t[0][h * E:(h + 1) * E, i * P:(i + 1) * P], mask[:, h * (TILES // 2) + i, :],
                                        ident[:, :], start=True, stop=True)
                    ins.then_inc(mask_turned, 1)

            def move_best(b):
                pe.wait_ge(best_ready, b + 1)
                pe.matmul(ps_t[1][0:E, 0:C], ident[:, E:P], best[:, :], start=True, stop=True).then_inc(best_moved, 1)

            pe.wait_ge(ident_steps, 2)
            for n in range(4):
                turn_x(n)
            for s in range(STEPS):
                step(s)
                if s == 0:
                    output_rows()
                for n in turned_after(s):
                    turn_x(n)
            pe.wait_ge(wo_lo_ready, KC)
            pe.wait_ge(const_ready, 2)

            def first_projections(b):
                project(b * TILES)
                project(b * TILES + 1)
                average(b, 0)
                average(b, 1)
                if b == 0:
                    turn_x(TILES)
                project(b * TILES + 2)
                project(b * TILES + 3)

            first_projections(0)
            pe.wait_ge(router_in, 16)
            for i in range(TILES):
                if i + 4 < TILES:
                    project(i + 4)
                if i:
                    router(i - 1)
                turn_xw(i)
                if i + 1 < TILES:
                    turn_x(TILES + 1 + i)
            router(TILES - 1)
            for s in range(STEPS, 2 * STEPS):
                step(s)
                if s == STEPS + 1:
                    turn_masks(0)
                if s == STEPS + 4:
                    move_best(0)
            first_projections(1)
            for i in range(TILES, 2 * TILES):
                if i + 4 < 2 * TILES:
                    project(i + 4)
                if i > TILES:
                    router(i - 1)
                turn_xw(i)
            router(2 * TILES - 1)
            def shared_gate_and_up(j):
                pe.wait_ge(xS_full, 16 * (j + 1))
                for w, (ps, ready) in enumerate(((ps_g[1], g_ready[2]), (ps_u[1], u_ready[2]))):
                    need(pe, (sg_ready, gu_ready)[w][2], j)
                    for c in range(KC):
                        ins = pe.matmul(ps[:, 0:I], xS[:, c, :], sh_gu[w][:, c, :],
                                        start=(c == 0), stop=(c == KC - 1))
                    ins.then_inc(ready, 1)

            turn_masks(1)
            pe.wait_ge(sh_full, 16 * 3)
            shared_gate_and_up(0)
            move_best(1)
            pe.wait_ge(tok_ready, 2)
            pe.transpose(ps_g[0][:, 0:E], tok2[:, :, :].rearrange("e a s -> e (a s)"), ident[0:E, 0:E]).then_inc(tok_turned, 1)
            pe.wait_ge(idx_ready, 3)

            def turn_tokens(j, u):
                pe.wait_ge(xg_full[u], 16 * (j + 1))
                if u == 0:
                    need(pe, guT_ready[2], j)
                else:
                    pe.wait_ge(xT_ready[0], j + 1)
                for c in range(KC):
                    ins = pe.transpose(ps_xt[:, c * P:(c + 1) * P], chunk(xg[u][:, 0:D], c), ident[:, :])
                ins.then_inc(xg_turned[u], 1)

            def group(j, r, last=False):
                def weights_in(j, u, k):
                    for n in range(2 * PIECES):
                        pe.wait_ge(w_full[n], j * 96 + 16 * (u * 3 + k + 1))

                def gate_and_up(u):
                    pe.wait_ge(xT_ready[u], j + 1)
                    for w, (ps, ready) in enumerate(((ps_g[0], g_ready[u]), (ps_u[0], u_ready[u]))):
                        weights_in(j, u, w)
                        need(pe, (sg_ready, gu_ready)[w][1 - u], j + u)
                        for c in range(KC):
                            for e in range(2):
                                ins = pe.matmul(ps[e * C:(e + 1) * C, 0:I], xT[u][:, c, e * C:(e + 1) * C],
                                                gate_up(r, u, e, w)[:, c, :], start=(c == 0), stop=(c == KC - 1))
                        ins.then_inc(ready, 1)

                def turn_gated(n, dst):
                    pe.wait_ge(gu_ready[n], j + 1)
                    if n == 0:
                        need(pe, guT_ready[1], j)
                    elif n == 1:
                        pe.wait_ge(guT_ready[0], j + 1)
                    else:
                        pe.wait_ge(xT_ready[1], j + 1)
                    for c in range(IC):
                        ins = pe.transpose(dst[:, c * P:(c + 1) * P], chunk(gu[n][:, :], c, IC), ident[:, :])
                    ins.then_inc(gu_turned[n], 1)

                def down_pair(u):
                    pe.wait_ge(guT_ready[u], j + 1)
                    weights_in(j, u, 2)
                    need(pe, yA_ready[1 - u], j + u)
                    need(pe, yB_ready[1 - u], j + u)
                    for c in range(IC):
                        for e in range(2):
                            ins = pe.matmul(ps_d[0][e * C:(e + 1) * C, :], guT[u][:, c, e * C:(e + 1) * C],
                                            down(r, u, e)[:, c, :], start=(c == 0), stop=(c == IC - 1))
                    ins.then_inc(d_ready[u], 1)

                def down_shared():
                    pe.wait_ge(guT_ready[2], j + 1)
                    need(pe, yS_ready, j)
                    for c in range(IC):
                        ins = pe.matmul(ps_d[1][:, :], guT[2][:, c, :], sh_dn[:, c, :],
                                        start=(c == 0), stop=(c == IC - 1))
                    ins.then_inc(d_ready[2], 1)

                if r or not isinstance(j, int) or j:
                    shared_gate_and_up(j)
                gate_and_up(0)
                turn_gated(2, ps_xt)
                turn_gated(0, ps_ht)
                down_shared()
                down_pair(0)
                if not last:
                    turn_tokens(j + 1, 0)
                gate_and_up(1)
                if not last:
                    turn_tokens(j + 1, 1)
                turn_gated(1, ps_ht)
                down_pair(1)

            for u in range(2):
                turn_tokens(0, u)
            group(0, 0)
            with pe.Fori(0, (GROUPS - 4) // 3) as i:
                for n in range(3):
                    group(i * 3 + (n + 1), (n + 1) % 3)
            for j in range(GROUPS - 3, GROUPS):
                group(j, j % 3, last=j == GROUPS - 1)


_ARGS = ["L0_attn_x", "L0_attn_Wr", "L0_attn_Wk", "L0_attn_Wv", "L0_attn_Wo", "L0_attn_decay", "L0_attn_gn_weight",
         "L0_attn_gn_bias", "L0_ffn_w_router", "L0_ffn_w_gate", "L0_ffn_w_up", "L0_ffn_w_down",
         "L0_ffn_w_sh_gate", "L0_ffn_w_sh_up", "L0_ffn_w_sh_down"]
_SWAPPED = {"L0_attn_Wr", "L0_attn_Wk", "L0_attn_Wv", "L0_attn_Wo", "L0_ffn_w_router"}


def kernel(**inputs):
    import numpy as _np
    import concourse.bacc as _bacc
    from concourse import mybir as _mybir
    from concourse.bass_utils import run_bass_kernel_spmd as _run

    nc = _bacc.Bacc("TRN2", target_bir_lowering=False, num_devices=1)
    arrays, args = {}, []
    for name in _ARGS:
        a = _np.asarray(inputs[name])
        if name in _SWAPPED:
            a = a.T
        if name == "L0_attn_x":
            a = a.reshape(-1, a.shape[-1])
        a = _np.ascontiguousarray(a)
        arrays[f"in_{name}"] = a
        args.append(nc.dram_tensor(f"in_{name}", a.shape, _mybir.dt.from_np(a.dtype), kind="ExternalInput").ap())
    shape = inputs["L0_attn_x"].shape
    out = nc.dram_tensor("out_dram", (shape[0] * shape[1], shape[2]), F32, kind="ExternalOutput").ap()
    moe_block(nc, *args, out)
    r = _run(nc, [arrays], core_ids=[0])
    return r.results[0]["out_dram"].reshape(shape)
```
